# Optimizing a Trainium2 kernel written in Bass

```python
import numpy as np
import jax
import jax.numpy as jnp

def _softmax(x, axis=-1):
    return jax.nn.softmax(x, axis=axis)

def _gelu(x):
    return jax.nn.gelu(x, approximate=True)

def _silu(x):
    return jax.nn.silu(x)

def _sigmoid(x):
    return jax.nn.sigmoid(x)

def _layernorm(x, axis=-1, eps=1e-05):
    m = jnp.mean(x, axis=axis, keepdims=True)
    v = jnp.var(x, axis=axis, keepdims=True)
    return (x - m) / jnp.sqrt(v + eps)

def _scatter_add(tgt, idx, src, axis=0):
    return tgt.at[idx].add(src)

def _segment_sum(src, seg, n):
    return jax.ops.segment_sum(src, seg, n)
kernel_name = 'mk_decoder_preln_d1_seqx_r8_d65315'

def setup_inputs(seed: int=0):
    np.random.seed(seed)
    _w = jnp.asarray

    def _rec_inputs():
        import jax
        import jax.numpy as jnp
        _rk = jax.random.key(seed)
        x = -0.0003929 + 0.9999 * jax.random.normal(jax.random.fold_in(_rk, 1), (16, 64, 128), jnp.float32)
        _lenS = 64 - jax.random.randint(jax.random.fold_in(_rk, 7), (16,), 0, max(1, 64 // 4) + 1, jnp.int32)
        _lenS2 = 64 - jax.random.randint(jax.random.fold_in(_rk, 8), (16,), 0, max(1, 64 // 4) + 1, jnp.int32)
        _ctx_1024P = jax.random.normal(jax.random.fold_in(_rk, 11), (16, 16, 128), jnp.float32)
        _ctx_1024c = jax.random.dirichlet(jax.random.fold_in(_rk, 511), 0.3 * jnp.ones((16,), jnp.float32), (16, 64))
        _ctx_1024t = jnp.einsum('bsk,bkd->bsd', _ctx_1024c, _ctx_1024P)
        _ctx_1024t = _ctx_1024t * jax.lax.rsqrt(jnp.mean(jnp.square(_ctx_1024t)) + 1e-12) * 0.953939
        ctx_1024 = 2.81802e-05 + 1.00001 * (_ctx_1024t + 0.3 * jax.random.normal(jax.random.fold_in(_rk, 611), (16, 64, 128), jnp.float32))
        return (x, ctx_1024)
    x, ctx_1024 = _rec_inputs()

    def _L0_attn_setup():
        import math
        import jax, jax.numpy as jnp
        import numpy as np
        HEADS = 16
        key = jax.random.key(seed)
        k1, k2, k3, k4, k5 = jax.random.split(key, 5)
        B, S, D = (2, 256, 128)
        return {'x': jax.random.normal(k1, (B, S, D), dtype=jnp.float32), 'Wqkv': jax.random.normal(k2, (3 * D, D), dtype=jnp.float32) * (1.0 / math.sqrt(D)), 'bqkv': jax.random.normal(k3, (3 * D,), dtype=jnp.float32) * 0.02, 'Wo': jax.random.normal(k4, (D, D), dtype=jnp.float32) * (1.0 / math.sqrt(D)), 'bo': jax.random.normal(k5, (D,), dtype=jnp.float32) * 0.02}
    _L0_attn_all = _L0_attn_setup()
    _L0_attn_in = {k: v for k, v in _L0_attn_all.items() if k in ('Wqkv', 'bqkv', 'Wo', 'bo')}
    del _L0_attn_all

    def _L0_xattn_setup():
        import jax, jax.numpy as jnp
        import numpy as np
        import math
        D_MODEL = 128
        N_HEADS = 16
        C = 1
        B, L = (8, 256)

        def _glorot(key, fan):
            lim = np.sqrt(6.0 / (fan + fan)).astype(np.float32)
            return jax.random.uniform(key, (fan, fan), jnp.float32, -lim, lim)
        key = jax.random.key(seed)
        ks = jax.random.split(key, 7)
        queries = jax.random.normal(ks[0], (B, L, D_MODEL), jnp.float32)
        keys = jax.random.normal(ks[1], (B, L, D_MODEL), jnp.float32)
        values = jax.random.normal(ks[2], (B, L, D_MODEL), jnp.float32)
        wq = _glorot(ks[3], D_MODEL)
        wk = _glorot(ks[4], D_MODEL)
        wv = _glorot(ks[5], D_MODEL)
        wo = _glorot(ks[6], D_MODEL)
        return {'queries': queries, 'keys': keys, 'values': values, 'wq': wq, 'wk': wk, 'wv': wv, 'wo': wo}
    _L0_xattn_all = _L0_xattn_setup()
    _L0_xattn_in = {k: v for k, v in _L0_xattn_all.items() if k in ('wq', 'wk', 'wv', 'wo')}
    del _L0_xattn_all

    def _L0_ffn_setup():
        import jax, jax.numpy as jnp
        import numpy as np
        DIM = 128
        NUM_EXPERTS = 8
        TOP_K = 2
        HIDDEN = 4 * DIM // TOP_K
        BS, SLEN = (1, 256)

        def _moe(x, gate_w, w_up, w_down, expert_bias):
            bs, slen, dim = x.shape
            xf = x.reshape(-1, dim)
            scores = jax.nn.sigmoid(xf @ gate_w.T)
            biased = scores + expert_bias
            _, sel = jax.lax.top_k(biased, TOP_K)
            top_scores = jnp.take_along_axis(scores, sel, axis=-1)

            def body(acc, ew):
                e, wu, wd = ew
                w_t = jnp.sum(jnp.where(sel == e, top_scores, 0.0), axis=-1)
                xe = xf * w_t[:, None]
                h = jnp.square(jax.nn.relu(xe @ wu.T))
                return (acc + h @ wd.T, None)
            out0 = jnp.zeros_like(xf)
            out, _ = jax.lax.scan(body, out0, (jnp.arange(NUM_EXPERTS), w_up, w_down))
            return out.reshape(bs, slen, dim)
        key = jax.random.key(seed)
        k0, k1, k2, k3 = jax.random.split(key, 4)
        x = jax.random.normal(k0, (BS, SLEN, DIM), dtype=jnp.float32)
        gate_w = jax.random.normal(k1, (NUM_EXPERTS, DIM), dtype=jnp.float32) * 0.02
        w_up = jax.random.normal(k2, (NUM_EXPERTS, HIDDEN, DIM), dtype=jnp.float32) * 0.02
        w_down = jax.random.normal(k3, (NUM_EXPERTS, DIM, HIDDEN), dtype=jnp.float32) * 0.02
        expert_bias = jnp.zeros((NUM_EXPERTS,), dtype=jnp.float32)
        return {'x': x, 'gate_w': gate_w, 'w_up': w_up, 'w_down': w_down, 'expert_bias': expert_bias}
    _L0_ffn_all = _L0_ffn_setup()
    _L0_ffn_in = {k: v for k, v in _L0_ffn_all.items() if k in ('gate_w', 'w_up', 'w_down', 'expert_bias')}
    del _L0_ffn_all
    return {'x': x, 'ctx_1024': ctx_1024, 'L0_attn_Wqkv': _L0_attn_in['Wqkv'], 'L0_attn_bqkv': _L0_attn_in['bqkv'], 'L0_attn_Wo': _L0_attn_in['Wo'], 'L0_attn_bo': _L0_attn_in['bo'], 'L0_xattn_wq': _L0_xattn_in['wq'], 'L0_xattn_wk': _L0_xattn_in['wk'], 'L0_xattn_wv': _L0_xattn_in['wv'], 'L0_xattn_wo': _L0_xattn_in['wo'], 'L0_ffn_gate_w': _L0_ffn_in['gate_w'], 'L0_ffn_w_up': _L0_ffn_in['w_up'], 'L0_ffn_w_down': _L0_ffn_in['w_down'], 'L0_ffn_expert_bias': _L0_ffn_in['expert_bias']}

def reference(x, ctx_1024, L0_attn_Wqkv, L0_attn_bqkv, L0_attn_Wo, L0_attn_bo, L0_xattn_wq, L0_xattn_wk, L0_xattn_wv, L0_xattn_wo, L0_ffn_gate_w, L0_ffn_w_up, L0_ffn_w_down, L0_ffn_expert_bias):
    import jax
    import jax.numpy as jnp

    def _L0_attn_ref(x, Wqkv, bqkv, Wo, bo):
        import math
        import jax, jax.numpy as jnp
        import numpy as np
        HEADS = 16
        B, S, D = x.shape
        H = HEADS
        hd = D // H
        qkv = x @ Wqkv.T + bqkv
        qkv = qkv.reshape(B, H, S, 3 * hd)
        q, k, v = jnp.split(qkv, 3, axis=-1)
        scores = jnp.einsum('bhsd,bhtd->bhst', q, k) * (1.0 / math.sqrt(hd))
        attn = jax.nn.softmax(scores, axis=-1)
        vals = jnp.einsum('bhst,bhtd->bhsd', attn, v)
        vals = vals.reshape(B, S, D)
        return vals @ Wo.T + bo

    def _L0_xattn_ref(queries, keys, values, wq, wk, wv, wo):
        import jax, jax.numpy as jnp
        import numpy as np
        import math
        D_MODEL = 128
        N_HEADS = 16
        C = 1
        B, L = (8, 256)

        def _glorot(key, fan):
            lim = np.sqrt(6.0 / (fan + fan)).astype(np.float32)
            return jax.random.uniform(key, (fan, fan), jnp.float32, -lim, lim)
        Bv, Lv, _ = queries.shape
        H = N_HEADS
        Dh = D_MODEL // N_HEADS
        Q = (queries @ wq).reshape(Bv, Lv, H, Dh).transpose(0, 2, 3, 1)
        K = (keys @ wk).reshape(Bv, Lv, H, Dh).transpose(0, 2, 3, 1)
        V = (values @ wv).reshape(Bv, Lv, H, Dh).transpose(0, 2, 3, 1)
        corr = jnp.fft.irfft(jnp.fft.rfft(Q, axis=-1) * jnp.conj(jnp.fft.rfft(K, axis=-1)), n=Lv, axis=-1)
        k_top = int(math.floor(C * math.log(Lv)))
        top_vals, top_idx = jax.lax.top_k(corr, k_top)
        w = jax.nn.softmax(top_vals, axis=-1)
        t = jnp.arange(Dh)
        out = jnp.zeros_like(V)
        for i in range(k_top):
            gather_idx = (t[None, None, :] - top_idx[..., i]) % Dh
            rolled = jnp.take_along_axis(V, gather_idx[..., None], axis=2)
            out = out + w[..., i, None] * rolled
        out = out.transpose(0, 2, 1, 3).reshape(Bv, Lv, D_MODEL)
        return out @ wo

    def _L0_ffn_ref(x, gate_w, w_up, w_down, expert_bias):
        import jax, jax.numpy as jnp
        import numpy as np
        DIM = 128
        NUM_EXPERTS = 8
        TOP_K = 2
        HIDDEN = 4 * DIM // TOP_K
        BS, SLEN = (1, 256)

        def _moe(x, gate_w, w_up, w_down, expert_bias):
            bs, slen, dim = x.shape
            xf = x.reshape(-1, dim)
            scores = jax.nn.sigmoid(xf @ gate_w.T)
            biased = scores + expert_bias
            _, sel = jax.lax.top_k(biased, TOP_K)
            top_scores = jnp.take_along_axis(scores, sel, axis=-1)

            def body(acc, ew):
                e, wu, wd = ew
                w_t = jnp.sum(jnp.where(sel == e, top_scores, 0.0), axis=-1)
                xe = xf * w_t[:, None]
                h = jnp.square(jax.nn.relu(xe @ wu.T))
                return (acc + h @ wd.T, None)
            out0 = jnp.zeros_like(xf)
            out, _ = jax.lax.scan(body, out0, (jnp.arange(NUM_EXPERTS), w_up, w_down))
            return out.reshape(bs, slen, dim)
        return _moe(x, gate_w, w_up, w_down, expert_bias)
    x = x + _L0_attn_ref(_layernorm(x, axis=-1), L0_attn_Wqkv, L0_attn_bqkv, L0_attn_Wo, L0_attn_bo)
    x = x + _L0_xattn_ref(_layernorm(x, axis=-1), ctx_1024, ctx_1024, L0_xattn_wq, L0_xattn_wk, L0_xattn_wv, L0_xattn_wo)
    x = x + _L0_ffn_ref(_layernorm(x, axis=-1), L0_ffn_gate_w, L0_ffn_w_up, L0_ffn_w_down, L0_ffn_expert_bias)
    return x

_drawn_inputs = setup_inputs


def setup_inputs(seed=0):
    import zlib

    import numpy as np

    out = dict(_drawn_inputs(seed))
    spreads = {'L0_ffn_expert_bias': (0.0, 0.8)}
    factors = {'L0_attn_bqkv': 2.886,
     'L0_attn_bo': 3.578,
     'L0_ffn_gate_w': 8.0,
     'L0_ffn_w_up': 8.0,
     'L0_ffn_w_down': 8.0}
    for name, (base, spread) in spreads.items():
        noise = np.random.default_rng([zlib.crc32(name.encode()), seed]).standard_normal(out[name].shape)
        drawn = base * np.exp(spread * noise) if base else spread * noise
        out[name] = jnp.asarray(drawn.astype(out[name].dtype))
    for name, factor in factors.items():
        out[name] = (out[name] * factor).astype(out[name].dtype)
    return out
```

```python
from contextlib import ExitStack

import concourse.bass as bass
from concourse import mybir

ALU = mybir.AluOpType
ACT = mybir.ActivationFunctionType
F32 = mybir.dt.float32
BF16 = mybir.dt.bfloat16
U32 = mybir.dt.uint32
AX = mybir.AxisListType

P = 128
D = 128
B, L = 16, 64
TILES = B * L // P
CHUNKS = TILES // 2
J, HD = 16, 8
QUAD = 4
GROUPS = 8
S = 64
NB = 4
NF = 32
TOP = 4
EXPERTS, HIDDEN = 8, 256
EPS = 1e-5
SCALE = float(HD) ** -0.5

W_K, W_V, W_O2, W_Q, W_O, W_GATE = 0, 128, 256, 384, 512, 640
R_BQKV, R_BO, R_EBIAS, R_LEN = 0, 384, 512, 520
C_ID = 0
C_FWD = 128
C_INV = 256
C_REL = C_INV + 3 * NB * L
C_HEAD = C_REL + 8
C_IOTA = C_HEAD + J
C_POW = C_IOTA + 8
C_LEN = C_POW + 2


def steps():
    stages = [
        ("xt", 0), ("qkv", 1), ("cdft", 2), ("cproj", 3), ("score", 4), ("mt", 5), ("vtr", 6), ("shift", 7), ("pv", 9),
        ("vt2", 11), ("wo", 12), ("dft", 13), ("qp", 14), ("corr", 15), ("g", 17), ("ov", 18), ("y2", 19), ("xt3", 20),
        ("gate", 21), ("wt", 23),
    ]
    skew = 4
    order = sorted((slot + skew * a, a, n, name) for n, (name, slot) in enumerate(stages) for a in range(CHUNKS))
    out = [(name, a) for _, a, _, name in order]
    last0 = out.index(("wt", 1)) + 1
    tail, merged, unit = out[last0:], out[:last0], 0
    for i, st in enumerate(tail):
        if i % 2 == 1 and unit < EXPERTS - 1:
            merged.append(("moe", unit))
            unit += 1
        merged.append(st)
    while unit < 2 * EXPERTS + 1:
        merged.append(("moe", unit))
        unit += 1
    return merged


STEPS = steps()


def numbered(uses):
    at = {}
    for name, a in STEPS:
        for part in range(uses.get(name, 0)):
            at[(name, a, part)] = len(at)
    return at


def decoder_layer(nc, x, ctxt, w_qkv, w_mid, w_up, w_down, rows, consts, sel, out):
    with ExitStack() as ctx:
        def sb(name, shape, dt=F32):
            return ctx.enter_context(nc.sbuf_tensor(name, shape, dt))

        def sem(name):
            return ctx.enter_context(nc.semaphore(name))

        x_sb = sb("x_sb", [P, TILES, D])
        c_sb = sb("c_sb", [P, TILES, D])
        x1 = sb("x1", [P, TILES, D])
        x2 = sb("x2", [P, TILES, D])
        xn = sb("xn", [P, 2, TILES, D])
        stat = sb("stat", [P, 3 * CHUNKS, 2, 6])
        mv = sb("mv", [P, 3 * CHUNKS, 2, 2])
        rstd = sb("rstd", [P, 3 * CHUNKS, 2])
        xt = sb("xt", [P, 2, 2 * P])
        wqkv_sb = sb("wqkv_sb", [P, 3 * D])
        wmid_sb = sb("wmid_sb", [P, W_GATE + EXPERTS])
        wup_sb = sb("wup_sb", [P, EXPERTS, HIDDEN])
        wdn_sb = sb("wdn_sb", [P, EXPERTS, 2, D])
        row_sb = sb("row_sb", [P, R_LEN])
        con = sb("con", [P, C_LEN])
        self32 = sb("self32", [3 * EXPERTS, EXPERTS * P])
        identb = sb("identb", [P, P], BF16)
        selb = sb("selb", [3 * EXPERTS, EXPERTS, P], BF16)
        nat = sb("nat", [P, 2, 3, J, 32])
        bd = sb("bd", [P, 3, CHUNKS * GROUPS, 2 * S])
        dense = sb("dense", [P, 2, 2, GROUPS, S])
        negm = sb("negm", [P, CHUNKS, QUAD, GROUPS])
        negmT = sb("negmT", [32, CHUNKS, 2 * S])
        prob = sb("prob", [P, 2, QUAD, GROUPS, S])
        vbd = sb("vbd", [P, 2, GROUPS, P])
        onat = sb("onat", [P, 2, J, 32])
        rden = sb("rden", [P, 2, J, 2])
        vals = sb("vals", [P, 2, 2, D])
        valsT = sb("valsT", [P, 2, 2 * P])
        cx = sb("cx", [P, 2, 4 * P])
        kv = sb("kv", [P, CHUNKS, 4 * P])
        qf = sb("qf", [P, 2, 2 * P])
        prod = sb("prod", [P, 2, 4, D])
        topv = sb("topv", [P, CHUNKS, NB, 8])
        topi = sb("topi", [P, CHUNKS, NB, 8], U32)
        topr = sb("topr", [P, CHUNKS, NB, 8], U32)
        dif = sb("dif", [P, CHUNKS, NB, TOP])
        ex = sb("ex", [P, CHUNKS, NB, TOP])
        exs = sb("exs", [P, CHUNKS, NB])
        exr = sb("exr", [P, CHUNKS, NB])
        wgt = sb("wgt", [P, CHUNKS, NB, TOP])
        hit = sb("hit", [P, CHUNKS, NB, 8, TOP])
        hitw = sb("hitw", [P, CHUNKS, NB, 8, TOP])
        w8 = sb("w8", [P, CHUNKS, NB, 8])
        mix = sb("mix", [P, 2, NB, J, 8])
        mixT = sb("mixT", [P, NB, D])
        ovT = sb("ovT", [P, 2, NB, HD, J // 2])
        xn3T = sb("xn3T", [P, TILES * P])
        eg = sb("eg", [P, CHUNKS, 2, EXPERTS])
        eg1 = sb("eg1", [P, CHUNKS, 2, EXPERTS])
        gate = sb("gate", [P, CHUNKS, 2, EXPERTS])
        biased = sb("biased", [P, CHUNKS, 2, EXPERTS])
        bestv = sb("bestv", [P, CHUNKS, 2, 8])
        besti = sb("besti", [P, CHUNKS, 2, 8], U32)
        pick = sb("pick", [P, CHUNKS, 2, EXPERTS, 2])
        picked = sb("picked", [P, CHUNKS, 2, EXPERTS])
        wtok = sb("wtok", [P, CHUNKS, 2, EXPERTS])
        rest = sb("rest", [P, CHUNKS, 2, 2, EXPERTS])
        wsplit = sb("wsplit", [P, CHUNKS, 2, 3 * EXPERTS], BF16)
        wT = sb("wT", [3 * EXPERTS, TILES * P], BF16)
        xe = c_sb[:].rearrange("p (i t) d -> p i (t d)", i=2)
        early = prob[:].rearrange("p i r h s -> p (i r) (h s)")
        hid, rel, accT = early[:, 0:4, :], early[:, 4:6, :], early[:, 6, :]
        fin = x_sb

        ps = ctx.enter_context(nc.psum_tensor("ps", [P, 8, 512], F32))
        score_ps = [ps[:, 0, :], ps[:, 1, :]]
        shift_ps = [ps[:, 2, :], ps[:, 3, :]]
        work_ps = [ps[:, 4, :], ps[:, 7, :]]
        turn_ps = ps[:, 5, :]
        side_ps = ps[:, 6, :]
        z_ps = [ps[:, 0, :], ps[:, 1, :], ps[:, 2, :]]
        wb_ps = ps[:, 3, :]
        acc_ps = [side_ps, turn_ps]

        turn_at = numbered({"xt": 1, "cdft": 1, "mt": 1, "vt2": 1, "dft": 1, "g": 1, "ov": 1, "xt3": 1, "gate": 1, "wt": 1})
        side_at = numbered({"cproj": 1, "vtr": 2})
        work_at = numbered({"qkv": 2, "pv": 1, "wo": 1, "qp": 1, "corr": 1, "y2": 1})
        n_work = len(work_at)

        ld_x = [sem(f"ld_x{a}") for a in range(CHUNKS)]
        ld_c = sem("ld_c")
        ld_id, ld_con, ld_wqkv, ld_mid, ld_up, ld_dn, ld_row, ld_sel = (
            sem(n) for n in ("ld_id", "ld_con", "ld_wqkv", "ld_mid", "ld_up", "ld_dn", "ld_row", "ld_sel"))
        zeroed = sem("zeroed")
        sel_ready = sem("sel_ready")
        id_bf = sem("id_bf")
        xb_ready = sem("xb_ready")
        stats_ready = sem("stats_ready")
        agg = sem("agg")
        veps_ready = sem("veps_ready")
        rstd_ready = sem("rstd_ready")
        norm_ready = sem("norm_ready")
        turn_full, turn_free = sem("turn_full"), sem("turn_free")
        side_full, side_free = sem("side_full"), sem("side_free")
        work_full, work_free = sem("work_full"), sem("work_free")
        score_full, score_free = sem("score_full"), sem("score_free")
        shift_full, shift_free = sem("shift_full"), sem("shift_free")
        nat_ready = sem("nat_ready")
        bd_ready = sem("bd_ready")
        dense_ready = sem("dense_ready")
        max_row = [sem(f"max_row{a}") for a in range(CHUNKS)]
        onat_ready = sem("onat_ready")
        rden_ready = sem("rden_ready")
        vals_ready = sem("vals_ready")
        x1_ready = sem("x1_ready")
        prod_ready = sem("prod_ready")
        prodc_ready = sem("prodc_ready")
        top_val = sem("top_val")
        dif_ready = sem("dif_ready")
        ex_ready = sem("ex_ready")
        tk = sem("tk")
        w8_ready = sem("w8_ready")
        mix_ready = sem("mix_ready")
        x2_ready = sem("x2_ready")
        split_ready = sem("split_ready")
        wb_full, wb_free = sem("wb_full"), sem("wb_free")
        z_full, z_free = sem("z_full"), sem("z_free")
        hid_ready = sem("hid_ready")
        down_done = sem("down_done")
        acct_ready = sem("acct_ready")
        fin_ready = sem("fin_ready")
        stored = sem("stored")

        ident = con[:, C_ID:C_ID + P]
        block = ctx.enter_context(nc.Block())

        @block.sync
        def _(sp):
            xv = x.rearrange("(t p) d -> p t d", p=P)
            ov = out.rearrange("(t p) d -> p t d", p=P)
            for a in range(CHUNKS):
                sp.dma_start(x_sb[:, 2 * a:2 * a + 2, :], xv[:, 2 * a:2 * a + 2, :]).then_inc(ld_x[a], 16)
            sp.dma_start(c_sb[:], ctxt.rearrange("(t p) d -> p t d", p=P)).then_inc(ld_c, 16)
            sp.dma_start(wup_sb[:].rearrange("p e h -> p (e h)"), w_up).then_inc(ld_up, 16)
            sp.dma_start(wdn_sb[:].rearrange("p e c n -> p (e c n)"), w_down).then_inc(ld_dn, 16)
            for name, a in STEPS:
                if name == "mt":
                    sp.wait_ge(turn_free, turn_at[("mt", a, 0)] + 1)
                    sp.wait_ge(dense_ready, 2 * (a + 1))
                    for r in range(QUAD):
                        for g in range(2):
                            row = 32 * r + 2 * HD + g
                            sp.dma_start(dense[row:row + 1, a % 2, 0, :, :],
                                         negmT[GROUPS * r:GROUPS * (r + 1), a, S * g:S * (g + 1)]).then_inc(max_row[a], 16)
            for hf in range(2):
                sp.wait_ge(fin_ready, hf + 1)
                sp.dma_start(ov[:, 4 * hf:4 * hf + 4, :], fin[:, 4 * hf:4 * hf + 4, :]).then_inc(stored, 16)
            sp.wait_ge(stored, 32)

        @block.gpsimd
        def _(pool):
            nc.gpsimd.memset(nat[:], 0.0).then_inc(zeroed, 1)
            pool.wait_ge(zeroed, 1)
            for g in range(2):
                nc.gpsimd.memset(nat[:, g, 1:3, :, 2 * HD + g:2 * HD + g + 1], 1.0).then_inc(zeroed, 1)
            pool.wait_ge(ld_id, 16)
            nc.gpsimd.tensor_copy(identb[:], ident).then_inc(id_bf, 1)
            pool.wait_ge(ld_sel, 16)
            nc.gpsimd.tensor_copy(selb[:].rearrange("k e p -> k (e p)"), self32[:]).then_inc(sel_ready, 1)

            def rsqrt(n):
                pool.wait_ge(stats_ready, 2 * (n + 1))
                if n == 0:
                    pool.wait_ge(ld_con, 16)
                nc.gpsimd.tensor_scalar(rstd[:, n, :], mv[:, n, :, 1], EPS, None, ALU.add).then_inc(veps_ready, 1)
                pool.wait_ge(veps_ready, n + 1)
                nc.gpsimd.tensor_tensor(rstd[:, n, :], rstd[:, n, :], con[:, C_POW:C_POW + 2], ALU.pow).then_inc(rstd_ready, 1)

            norms = 0
            for name, a in STEPS:
                if name in ("xt", "dft", "xt3"):
                    rsqrt(norms)
                    norms += 1
                if name == "xt" and a == 0:
                    pool.wait_ge(ld_row, 16)
                    for q in range(CHUNKS):
                        pool.wait_ge(ld_x[q], 16)
                    nc.gpsimd.tensor_tensor(x1[:], x_sb[:], row_sb[:, R_BO:R_BO + D].unsqueeze(1).broadcast_to([P, TILES, D]),
                                            ALU.add).then_inc(xb_ready, 1)
                if name == "qkv":
                    pool.wait_ge(bd_ready, 6 * (a + 1))
                    if a >= 2:
                        pool.wait_ge(shift_full, 2 * (a - 1))
                    for qk in range(2):
                        own = bd[:, qk, GROUPS * a:GROUPS * (a + 1), :]
                        nc.gpsimd.tensor_tensor(dense[:, a % 2, qk], own[:, :, 0:S], own[:, :, S:2 * S],
                                                ALU.add).then_inc(dense_ready, 1)
                if name == "corr":
                    pool.wait_ge(w8_ready, a + 1)
                    if a >= 2:
                        pool.wait_ge(turn_full, turn_at[("g", a - 2, 0)] + 1)
                    for b in range(NB):
                        last = nc.gpsimd.tensor_tensor(
                            mix[:, a % 2, b], w8[:, a, b, :].unsqueeze(1).broadcast_to([P, J, 8]),
                            con[:, C_HEAD:C_HEAD + J].unsqueeze(2).broadcast_to([P, J, 8]), ALU.mult)
                    last.then_inc(mix_ready, 1)

        @block.scalar
        def _(act):
            act.dma_start(con[:, 0:P], consts[:, 0:P]).then_inc(ld_id, 16)
            act.dma_start(wqkv_sb[:], w_qkv).then_inc(ld_wqkv, 16)
            act.dma_start(row_sb[:], rows.partition_broadcast(P)).then_inc(ld_row, 16)
            act.dma_start(con[:, P:C_LEN], consts[:, P:C_LEN]).then_inc(ld_con, 16)
            act.dma_start(wmid_sb[:], w_mid).then_inc(ld_mid, 16)
            act.dma_start(self32[:], sel).then_inc(ld_sel, 16)

            def turn(name, a, dst, src):
                act.wait_ge(turn_full, turn_at[(name, a, 0)] + 1)
                nc.scalar.copy(dst, src).then_inc(turn_free, 1)

            def side(name, a, part, dst, src):
                act.wait_ge(side_full, side_at[(name, a, part)] + 1)
                nc.scalar.copy(dst, src).then_inc(side_free, 1)

            for name, a in STEPS:
                if name == "xt":
                    if a >= 2:
                        act.wait_ge(work_full, work_at[("qkv", a - 2, 1)] + 1)
                    turn(name, a, xt[:, a % 2, :], turn_ps[:, 0:2 * P])
                if name == "cdft":
                    if a >= 2:
                        act.wait_ge(side_full, side_at[("cproj", a - 2, 0)] + 1)
                    turn(name, a, cx[:, a % 2, :], turn_ps)
                if name == "cproj":
                    side(name, a, 0, kv[:, a, :], side_ps)
                if name == "mt":
                    turn(name, a, negmT[:, a, :], turn_ps[0:32, 0:P])
                if name == "vtr":
                    for half in range(2):
                        if a >= 2:
                            act.wait_ge(work_full, work_at[("pv", a - 2, 0)] + 1)
                        side(name, a, half, vbd[:, a % 2, 4 * half:4 * half + 4, :],
                             side_ps.rearrange("p (h n) -> p h n", n=P))
                if name == "shift":
                    for r in range(QUAD):
                        act.wait_ge(shift_full, 2 * a + r // 2 + 1)
                        if a >= 2:
                            act.wait_ge(work_full, work_at[("pv", a - 2, 0)] + 1)
                        nc.scalar.activation(prob[:, a % 2, r], shift_ps[r % 2].rearrange("p (h s) -> p h s", s=S), ACT.Exp,
                                             scale=SCALE).then_inc(shift_free, 1)
                if name == "vt2":
                    if a >= 2:
                        act.wait_ge(work_full, work_at[("wo", a - 2, 0)] + 1)
                    turn(name, a, valsT[:, a % 2, :], turn_ps[:, 0:2 * P])
                if name == "dft":
                    if a >= 2:
                        act.wait_ge(work_full, work_at[("qp", a - 2, 0)] + 1)
                    turn(name, a, qf[:, a % 2, :], turn_ps[:, 0:2 * P])
                if name == "corr":
                    act.wait_ge(dif_ready, a + 1)
                    nc.scalar.activation(ex[:, a], dif[:, a], ACT.Exp).then_inc(ex_ready, 1)
                if name == "g":
                    if a >= 1:
                        act.wait_ge(turn_full, turn_at[("ov", a - 1, 0)] + 1)
                    turn(name, a, mixT[:], turn_ps.rearrange("p (b n) -> p b n", n=D))
                if name == "ov":
                    if a >= 2:
                        act.wait_ge(work_full, work_at[("y2", a - 2, 0)] + 1)
                    turn(name, a, ovT[:, a % 2].rearrange("p b d h -> p b h d"),
                         turn_ps[:, 0:NB * L].rearrange("p (b h d) -> p b h d", b=NB, d=HD))
                if name == "xt3":
                    turn(name, a, xn3T[:, 2 * P * a:2 * P * (a + 1)], turn_ps[:, 0:2 * P])
                if name == "gate":
                    act.wait_ge(turn_full, turn_at[(name, a, 0)] + 1)
                    nc.scalar.activation(eg[:, a].rearrange("p t e -> p (t e)"), turn_ps[:, 0:2 * EXPERTS], ACT.Exp,
                                         scale=-1.0).then_inc(turn_free, 1)
                if name == "wt":
                    turn(name, a, wT[:, 2 * P * a:2 * P * (a + 1)], turn_ps.bitcast(BF16)[0:3 * EXPERTS, 0:2 * P])
                if name == "moe" and a < 2 * EXPERTS:
                    for c in range(2):
                        k = 2 * a + c
                        act.wait_ge(z_full, k + 1)
                        if k >= 2:
                            act.wait_ge(hid_ready, k - 1)
                        nc.scalar.activation(rel[:, k % 2, :], z_ps[k % 3], ACT.Relu).then_inc(z_free, 1)
                if name == "moe" and a in (EXPERTS, 2 * EXPERTS):
                    hf = a // EXPERTS - 1
                    act.wait_ge(down_done, EXPERTS * (hf + 1))
                    if hf:
                        act.wait_ge(work_full, n_work + 1)
                    nc.scalar.copy(accT, acc_ps[hf]).then_inc(acct_ready, 1)

        @block.vector
        def _(dve):
            chain = [0]

            def link(ins):
                chain[0] += 1
                ins.then_inc(tk, 1)
                dve.wait_ge(tk, chain[0])

            def stats(n, src, a):
                for t in range(2):
                    nc.vector.bn_stats(stat[:, n, t, :], src[:, 2 * a + t, :]).then_inc(agg, 1)
                for t in range(2):
                    dve.wait_ge(agg, 2 * n + t + 1)
                    nc.vector.bn_aggr(mv[:, n, t, :], stat[:, n, t, :]).then_inc(stats_ready, 1)

            def normalise(n, dst, src, a):
                dve.wait_ge(rstd_ready, n + 1)
                dve.wait_ge(stats_ready, 2 * (n + 1))
                for t in range(2):
                    nc.vector.tensor_scalar(dst[:, 2 * a + t, :], src[:, 2 * a + t, :], mv[:, n, t, 0:1], rstd[:, n, t:t + 1],
                                            ALU.subtract, ALU.mult).then_inc(norm_ready, 1)

            def work(name, a, part=0):
                use = work_at[(name, a, part)]
                dve.wait_ge(work_full, use + 1)
                return work_ps[use % 2]

            def expert_input(i):
                hf = i // EXPERTS
                dve.wait_ge(wb_full, i + 1)
                if i >= 2:
                    dve.wait_ge(z_full, 2 * (i - 1))
                dve.wait_ge(turn_free, turn_at[("xt3", 2 * hf + 1, 0)] + 1)
                nc.vector.tensor_tensor(xe[:, i % 2, :], wb_ps, xn3T[:, 4 * P * hf:4 * P * (hf + 1)], ALU.mult).then_inc(wb_free, 1)

            norms = 0
            for name, a in STEPS:
                if name == "xt":
                    dve.wait_ge(ld_x[a], 16)
                    stats(norms, x_sb, a)
                    normalise(norms, xn[:, 0], x_sb, a)
                    norms += 1
                if name == "qkv":
                    if a == 0:
                        dve.wait_ge(zeroed, 3)
                        dve.wait_ge(ld_row, 16)
                    for t in range(2):
                        if a > 0:
                            dve.wait_ge(bd_ready, 6 * (a - 1) + 3 * (t + 1))
                        nc.vector.tensor_tensor(
                            nat[:, t, :, :, HD * t:HD * (t + 1)].rearrange("p c j d -> p (c j) d"),
                            work(name, a, t)[:, 0:3 * D].rearrange("p (c d) -> p c d", d=HD),
                            row_sb[:, R_BQKV:R_BQKV + 3 * D].rearrange("p (c d) -> p c d", d=HD), ALU.add).then_inc(work_free, 1)
                        dve.wait_ge(work_free, work_at[(name, a, t)] + 1)
                        for c in range(3):
                            nc.vector.transpose(
                                bd[:, c, GROUPS * a:GROUPS * (a + 1), S * t:S * (t + 1)].rearrange("p h (j r) -> p j h r", j=J),
                                nat[:, t, c, :, :]).then_inc(bd_ready, 1)
                if name == "score":
                    for r in range(QUAD):
                        dve.wait_ge(score_full, 2 * a + r // 2 + 1)
                        nc.vector.tensor_reduce(negm[:, a, r, :], score_ps[r % 2].rearrange("p (h s) -> p h s", s=S), AX.X, ALU.max,
                                                negate=True).then_inc(score_free, 1)
                if name == "pv":
                    nc.vector.transpose(onat[:, a % 2], work(name, a).rearrange("p (h j r) -> p j h r", h=GROUPS, j=J)).then_inc(work_free, 1)
                    dve.wait_ge(work_free, work_at[(name, a, 0)] + 1)
                    nc.vector.reciprocal(rden[:, a % 2], onat[:, a % 2, :, 2 * HD:2 * HD + 2]).then_inc(rden_ready, 1)
                    dve.wait_ge(rden_ready, a + 1)
                    if a >= 2:
                        dve.wait_ge(turn_full, turn_at[("vt2", a - 2, 0)] + 1)
                    for g in range(2):
                        nc.vector.tensor_tensor(
                            vals[:, a % 2, g].rearrange("p (j d) -> p j d", d=HD), onat[:, a % 2, :, HD * g:HD * (g + 1)],
                            rden[:, a % 2, :, g:g + 1].broadcast_to([P, J, HD]), ALU.mult).then_inc(vals_ready, 1)
                if name == "wo":
                    if a == 0:
                        dve.wait_ge(xb_ready, 1)
                    both = x1[:, 2 * a:2 * a + 2, :]
                    nc.vector.tensor_tensor(both, work(name, a)[:, 0:2 * D].rearrange("p (t n) -> p t n", n=D), both,
                                            ALU.add).then_inc(work_free, 1)
                    dve.wait_ge(work_free, work_at[(name, a, 0)] + 1)
                if name == "dft":
                    stats(norms, x1, a)
                    normalise(norms, xn[:, 1], x1, a)
                    norms += 1
                if name == "qp":
                    if a >= 2:
                        dve.wait_ge(work_full, work_at[("corr", a - 2, 0)] + 1)
                    dve.wait_ge(side_free, side_at[("cproj", a, 0)] + 1)
                    spec = work(name, a)
                    nc.vector.tensor_tensor(prod[:, a % 2, 0:2, :], spec[:, 0:2 * D].rearrange("p (i c) -> p i c", c=D),
                                            kv[:, a, 0:2 * D].rearrange("p (i c) -> p i c", c=D), ALU.mult).then_inc(prod_ready, 1)
                    nc.vector.tensor_tensor(prod[:, a % 2, 3, :], spec[:, 0:D], kv[:, a, D:2 * D], ALU.mult).then_inc(prodc_ready, 1)
                    nc.vector.tensor_tensor(prod[:, a % 2, 2, :], spec[:, D:2 * D], kv[:, a, 0:D], ALU.mult).then_inc(work_free, 1)
                    dve.wait_ge(prodc_ready, 2 * a + 1)
                    dve.wait_ge(work_free, work_at[(name, a, 0)] + 1)
                    nc.vector.tensor_tensor(prod[:, a % 2, 2, :], prod[:, a % 2, 2, :], prod[:, a % 2, 3, :],
                                            ALU.subtract).then_inc(prodc_ready, 1)
                if name == "corr":
                    corr = work(name, a)[:, 0:NB * L].rearrange("p (b s) -> p b s", s=L)
                    for b in range(NB):
                        nc.vector.max(topv[:, a, b, :], corr[:, b, :]).then_inc(top_val, 1)
                    for b in range(NB):
                        dve.wait_ge(top_val, NB * a + b + 1)
                        last = nc.vector.max_index(topi[:, a, b, :], topv[:, a, b, :], corr[:, b, :])
                    last.then_inc(work_free, 1)
                    dve.wait_ge(work_free, work_at[(name, a, 0)] + 1)
                    nc.vector.tensor_tensor(dif[:, a], topv[:, a, :, 0:TOP], topv[:, a, :, 0:1].broadcast_to([P, NB, TOP]),
                                            ALU.subtract).then_inc(dif_ready, 1)
                    link(nc.vector.tensor_single_scalar(topr[:, a], topi[:, a], HD - 1, ALU.bitwise_and))
                    if a == 0:
                        dve.wait_ge(ld_con, 16)
                    for b in range(NB):
                        last = nc.vector.tensor_tensor(
                            hit[:, a, b], topr[:, a, b, 0:TOP].unsqueeze(1).broadcast_to([P, 8, TOP]),
                            con[:, C_REL:C_REL + 8].unsqueeze(2).broadcast_to([P, 8, TOP]), ALU.is_equal)
                        if b < NB - 1:
                            link(last)
                    link(last)
                    dve.wait_ge(ex_ready, a + 1)
                    link(nc.vector.tensor_reduce(exs[:, a], ex[:, a], AX.X, ALU.add))
                    link(nc.vector.reciprocal(exr[:, a], exs[:, a]))
                    link(nc.vector.tensor_tensor(wgt[:, a], ex[:, a], exr[:, a].unsqueeze(2).broadcast_to([P, NB, TOP]), ALU.mult))
                    link(nc.vector.tensor_tensor(hitw[:, a], hit[:, a], wgt[:, a].unsqueeze(2).broadcast_to([P, NB, 8, TOP]), ALU.mult))
                    nc.vector.tensor_reduce(w8[:, a], hitw[:, a], AX.X, ALU.add).then_inc(w8_ready, 1)
                if name == "y2":
                    dve.wait_ge(work_free, work_at[("wo", a, 0)] + 1)
                    nc.vector.tensor_tensor(x2[:, 2 * a:2 * a + 2, :], work(name, a)[:, 0:2 * D].rearrange("p (t n) -> p t n", n=D),
                                            x1[:, 2 * a:2 * a + 2, :], ALU.add).then_inc(work_free, 1)
                    dve.wait_ge(work_free, work_at[(name, a, 0)] + 1)
                if name == "xt3":
                    stats(norms, x2, a)
                    dve.wait_ge(turn_full, turn_at[("xt", a, 0)] + 1)
                    normalise(norms, xn[:, 0], x2, a)
                    norms += 1
                if name == "gate":
                    dve.wait_ge(turn_free, turn_at[(name, a, 0)] + 1)
                    link(nc.vector.tensor_scalar(eg1[:, a], eg[:, a], 1.0, None, ALU.add))
                    link(nc.vector.reciprocal(gate[:, a], eg1[:, a]))
                    link(nc.vector.tensor_tensor(biased[:, a], gate[:, a],
                                                 row_sb[:, R_EBIAS:R_EBIAS + EXPERTS].unsqueeze(1).broadcast_to([P, 2, EXPERTS]), ALU.add))
                    for t in range(2):
                        link(nc.vector.max(bestv[:, a, t], biased[:, a, t]))
                        link(nc.vector.max_index(besti[:, a, t], bestv[:, a, t], biased[:, a, t]))
                    for t in range(2):
                        link(nc.vector.tensor_tensor(pick[:, a, t], besti[:, a, t, 0:2].unsqueeze(1).broadcast_to([P, EXPERTS, 2]),
                                                     con[:, C_IOTA:C_IOTA + 8].unsqueeze(2).broadcast_to([P, EXPERTS, 2]), ALU.is_equal))
                    link(nc.vector.tensor_reduce(picked[:, a], pick[:, a], AX.X, ALU.add))
                    link(nc.vector.tensor_tensor(wtok[:, a], picked[:, a], gate[:, a], ALU.mult))
                    part = [wsplit[:, a, :, EXPERTS * i:EXPERTS * (i + 1)] for i in range(3)]
                    link(nc.vector.tensor_copy(part[0], wtok[:, a]))
                    link(nc.vector.tensor_tensor(rest[:, a, 0], wtok[:, a], part[0], ALU.subtract))
                    link(nc.vector.tensor_copy(part[1], rest[:, a, 0]))
                    link(nc.vector.tensor_tensor(rest[:, a, 1], rest[:, a, 0], part[1], ALU.subtract))
                    nc.vector.tensor_copy(part[2], rest[:, a, 1]).then_inc(split_ready, 1)
                if name == "moe":
                    if a == 0:
                        expert_input(0)
                    if a + 1 < 2 * EXPERTS:
                        expert_input(a + 1)
                    if a < 2 * EXPERTS:
                        for c in range(2):
                            k = 2 * a + c
                            dve.wait_ge(z_free, k + 1)
                            if a >= 2:
                                dve.wait_ge(down_done, a - 1)
                            nc.vector.tensor_tensor(hid[:, k % 4, :], rel[:, k % 2, :], rel[:, k % 2, :], ALU.mult).then_inc(hid_ready, 1)
                    if a in (EXPERTS + 1, 2 * EXPERTS):
                        hf = a // (2 * EXPERTS)
                        dve.wait_ge(work_full, n_work + hf + 1)
                        nc.vector.tensor_tensor(fin[:, 4 * hf:4 * hf + 4, :],
                                                work_ps[(n_work + hf) % 2].rearrange("p (t n) -> p t n", n=D),
                                                x2[:, 4 * hf:4 * hf + 4, :], ALU.add).then_inc(fin_ready, 1)

        @block.tensor
        def _(pe):
            def bank(name, a, part=0):
                use = work_at[(name, a, part)]
                if use >= 2:
                    pe.wait_ge(work_free, use - 1)
                return work_ps[use % 2]

            def turn_bank(name, a):
                use = turn_at[(name, a, 0)]
                if use:
                    pe.wait_ge(turn_free, use)
                return turn_ps

            def side_bank(name, a, part):
                use = side_at[(name, a, part)]
                if use:
                    pe.wait_ge(side_free, use)
                return side_ps

            def turned(name, a):
                pe.wait_ge(turn_free, turn_at[(name, a, 0)] + 1)

            mm = nc.tensor.matmul
            norms = 0

            def broadcast(i):
                hf, e = divmod(i, EXPERTS)
                if i == 0:
                    pe.wait_ge(sel_ready, 1)
                    pe.wait_ge(shift_free, QUAD * CHUNKS)
                if i:
                    pe.wait_ge(wb_free, i)
                turned("wt", 2 * hf + 1)
                mm(wb_ps, selb[:, e, :], wT[:, 4 * P * hf:4 * P * (hf + 1)], start=True, stop=True).then_inc(wb_full, 1)

            for name, a in STEPS:
                if name in ("xt", "dft", "xt3"):
                    norms += 1
                if name in ("xt", "xt3"):
                    if name == "xt" and a == 0:
                        pe.wait_ge(ld_id, 16)
                    pe.wait_ge(norm_ready, 2 * norms)
                    ps_t = turn_bank(name, a)
                    for t in range(2):
                        last = nc.tensor.transpose(ps_t[:, P * t:P * (t + 1)], xn[:, 0, 2 * a + t, :], ident)
                    last.then_inc(turn_full, 1)
                if name == "qkv":
                    if a == 0:
                        pe.wait_ge(ld_wqkv, 16)
                    turned("xt", a)
                    for t in range(2):
                        mm(bank(name, a, t)[:, 0:3 * D], xt[:, a % 2, P * t:P * (t + 1)], wqkv_sb[:], start=True,
                           stop=True).then_inc(work_full, 1)
                if name == "cdft":
                    if a == 0:
                        pe.wait_ge(ld_c, 16)
                        pe.wait_ge(ld_con, 16)
                    ps_t = turn_bank(name, a)
                    spec = ps_t[:, 0:2 * P].rearrange("p (i t f) -> p i t f", i=2, t=2)
                    for t in range(2):
                        mm(spec[:, :, t, :], c_sb[:, 2 * a + t, :], con[:, C_FWD:C_FWD + 2 * 2 * NF].rearrange("p (i f) -> p i f", i=2),
                           start=True, stop=True)
                        last = nc.tensor.transpose(ps_t[:, 2 * P + P * t:2 * P + P * (t + 1)], c_sb[:, 2 * a + t, :], ident)
                    last.then_inc(turn_full, 1)
                if name == "cproj":
                    if a == 0:
                        pe.wait_ge(ld_mid, 16)
                    turned("cdft", a)
                    ps_s = side_bank(name, a, 0)
                    for i in range(2):
                        mm(ps_s[:, D * i:D * (i + 1)], cx[:, a % 2, P * i:P * (i + 1)], wmid_sb[:, W_K:W_K + D], start=True, stop=True)
                    mm(ps_s[:, 2 * P:4 * P], wmid_sb[:, W_V:W_V + D], cx[:, a % 2, 2 * P:4 * P], start=True,
                       stop=True).then_inc(side_full, 1)
                if name == "score":
                    pe.wait_ge(dense_ready, 2 * (a + 1))
                    for pair in range(2):
                        n = 2 * a + pair
                        if n:
                            pe.wait_ge(score_free, 2 * n)
                        for h in range(GROUPS):
                            for i in range(2):
                                q = 32 * (2 * pair + i)
                                last = mm(score_ps[i][:, S * h:S * (h + 1)], bd[q:q + 32, 0, GROUPS * a + h, :],
                                          dense[q:q + 32, a % 2, 1, h, :], start=True, stop=True)
                        last.then_inc(score_full, 1)
                if name == "mt":
                    pe.wait_ge(score_free, QUAD * (a + 1))
                    ps_t = turn_bank(name, a)
                    nc.tensor.transpose(ps_t[0:32, 0:P], negm[:, a].rearrange("p r h -> p (r h)"), ident).then_inc(turn_full, 1)
                if name == "shift":
                    pe.wait_ge(max_row[a], 16 * 2 * QUAD)
                    for pair in range(2):
                        n = 2 * a + pair
                        if n:
                            pe.wait_ge(shift_free, 2 * n)
                        for h in range(GROUPS):
                            for i in range(2):
                                q = 32 * (2 * pair + i)
                                last = mm(shift_ps[i][:, S * h:S * (h + 1)], bd[q:q + 32, 1, GROUPS * a + h, :],
                                          dense[q:q + 32, a % 2, 0, h, :], start=True, stop=True)
                        last.then_inc(shift_full, 1)
                if name == "vtr":
                    pe.wait_ge(bd_ready, 6 * (a + 1))
                    for half in range(2):
                        ps_s = side_bank(name, a, half)
                        for h in range(4):
                            last = nc.tensor.transpose(ps_s[:, P * h:P * (h + 1)], bd[:, 2, GROUPS * a + 4 * half + h, :], ident)
                        last.then_inc(side_full, 1)
                if name == "pv":
                    pe.wait_ge(side_free, side_at[("vtr", a, 1)] + 1)
                    o_ps = bank(name, a)
                    for r in range(QUAD):
                        pe.wait_ge(shift_free, QUAD * a + r + 1)
                        for h in range(GROUPS):
                            last = mm(o_ps[32 * r:32 * r + 32, S * h:S * (h + 1)], vbd[:, a % 2, h, 32 * r:32 * r + 32],
                                      prob[:, a % 2, r, h, :], start=True, stop=True)
                    last.then_inc(work_full, 1)
                if name == "vt2":
                    pe.wait_ge(vals_ready, 2 * (a + 1))
                    ps_t = turn_bank(name, a)
                    for t in range(2):
                        last = nc.tensor.transpose(ps_t[:, P * t:P * (t + 1)], vals[:, a % 2, t, :], ident)
                    last.then_inc(turn_full, 1)
                if name == "wo":
                    turned("vt2", a)
                    y_ps = bank(name, a)
                    for t in range(2):
                        last = mm(y_ps[:, D * t:D * (t + 1)], valsT[:, a % 2, P * t:P * (t + 1)], wmid_sb[:, W_O:W_O + D],
                                  start=True, stop=True)
                    last.then_inc(work_full, 1)
                if name == "dft":
                    pe.wait_ge(norm_ready, 2 * norms)
                    ps_t = turn_bank(name, a)
                    spec = ps_t[:, 0:2 * P].rearrange("p (i t f) -> p i t f", i=2, t=2)
                    for t in range(2):
                        last = mm(spec[:, :, t, :], xn[:, 1, 2 * a + t, :],
                                  con[:, C_FWD:C_FWD + 2 * 2 * NF].rearrange("p (i f) -> p i f", i=2), start=True, stop=True)
                    last.then_inc(turn_full, 1)
                if name == "qp":
                    turned("dft", a)
                    q_ps = bank(name, a)
                    for i in range(2):
                        last = mm(q_ps[:, D * i:D * (i + 1)], qf[:, a % 2, P * i:P * (i + 1)], wmid_sb[:, W_Q:W_Q + D],
                                  start=True, stop=True)
                    last.then_inc(work_full, 1)
                if name == "corr":
                    pe.wait_ge(prod_ready, a + 1)
                    pe.wait_ge(prodc_ready, 2 * (a + 1))
                    c_ps = bank(name, a)
                    for i in range(3):
                        last = mm(c_ps[:, 0:NB * L], prod[:, a % 2, i, :], con[:, C_INV + NB * L * i:C_INV + NB * L * (i + 1)],
                                  start=(i == 0), stop=(i == 2))
                    last.then_inc(work_full, 1)
                if name == "g":
                    pe.wait_ge(mix_ready, a + 1)
                    ps_t = turn_bank(name, a)
                    for b in range(NB):
                        last = nc.tensor.transpose(ps_t[:, D * b:D * (b + 1)], mix[:, a % 2, b].rearrange("p h e -> p (h e)"), ident)
                    last.then_inc(turn_full, 1)
                if name == "ov":
                    turned("g", a)
                    ps_t = turn_bank(name, a)
                    for b in range(NB):
                        for odd in range(2):
                            last = mm(ps_t[L * odd:L * (odd + 1), L * b:L * (b + 1)], kv[:, a, 2 * P + L * b:2 * P + L * (b + 1)],
                                      mixT[:, b, :].rearrange("p (h o d) -> p o h d", o=2, d=HD)[:, odd], start=True, stop=True)
                    last.then_inc(turn_full, 1)
                if name == "y2":
                    turned("ov", a)
                    y_ps = bank(name, a)
                    for t in range(2):
                        last = mm(y_ps[:, D * t:D * (t + 1)], ovT[:, a % 2, 2 * t:2 * t + 2].rearrange("p b d h -> p (b d h)"),
                                  wmid_sb[:, W_O2:W_O2 + D], start=True, stop=True)
                    last.then_inc(work_full, 1)
                if name == "gate":
                    turned("xt3", a)
                    ps_t = turn_bank(name, a)
                    for t in range(2):
                        last = mm(ps_t[:, EXPERTS * t:EXPERTS * (t + 1)], xn3T[:, P * (2 * a + t):P * (2 * a + t + 1)],
                                  wmid_sb[:, W_GATE:W_GATE + EXPERTS], start=True, stop=True)
                    last.then_inc(turn_full, 1)
                if name == "wt":
                    pe.wait_ge(split_ready, a + 1)
                    ps_t = turn_bank(name, a).bitcast(BF16)
                    if a == 0:
                        pe.wait_ge(id_bf, 1)
                    for t in range(2):
                        last = nc.tensor.transpose(ps_t[0:3 * EXPERTS, P * t:P * (t + 1)], wsplit[:, a, t, :], identb[:])
                    last.then_inc(turn_full, 1)
                if name == "moe":
                    if a == 0:
                        pe.wait_ge(ld_up, 16)
                        pe.wait_ge(ld_dn, 16)
                        pe.wait_ge(score_free, QUAD * CHUNKS)
                        broadcast(0)
                    if a + 1 < 2 * EXPERTS:
                        broadcast(a + 1)
                    if a < 2 * EXPERTS:
                        pe.wait_ge(wb_free, a + 1)
                        for c in range(2):
                            k = 2 * a + c
                            if k >= 3:
                                pe.wait_ge(z_free, k - 2)
                            up = mm(z_ps[k % 3], wup_sb[:, a % EXPERTS, P * c:P * (c + 1)], xe[:, a % 2, :], start=True, stop=True)
                            up.then_inc(z_full, 1)
                    if a > 0:
                        i = a - 1
                        hf, e = divmod(i, EXPERTS)
                        if e == 0:
                            if hf == 0:
                                pe.wait_ge(side_free, len(side_at))
                            else:
                                pe.wait_ge(turn_free, len(turn_at))
                        for c in range(2):
                            pe.wait_ge(hid_ready, 2 * i + c + 1)
                            dn = mm(acc_ps[hf], wdn_sb[:, e, c, :], hid[:, (2 * i + c) % 4, :], start=(e == 0 and c == 0),
                                    stop=(e == EXPERTS - 1 and c == 1))
                        dn.then_inc(down_done, 1)
                    if a in (EXPERTS + 1, 2 * EXPERTS):
                        hf = a // (2 * EXPERTS)
                        pe.wait_ge(acct_ready, hf + 1)
                        use = n_work + hf
                        if hf == 0:
                            pe.wait_ge(work_free, n_work)
                        for t in range(4):
                            last = nc.tensor.transpose(work_ps[use % 2][:, P * t:P * (t + 1)], accT[:, P * t:P * (t + 1)], ident)
                        last.then_inc(work_full, 1)


def constants():
    import numpy as np
    con = np.zeros((P, C_LEN), np.float64)
    con[:, C_ID:C_ID + P] = np.eye(P)
    l, f = np.arange(L), np.arange(NF)
    ang = 2 * np.pi * np.outer(l, f) / L
    alt = np.where(l % 2 == 0, 1.0, -1.0)
    re, im = np.cos(ang), -np.sin(ang)
    im[:, 0] = alt
    for b in range(2):
        con[L * b:L * (b + 1), C_FWD + NF * b:C_FWD + NF * (b + 1)] = re
        con[L * b:L * (b + 1), C_FWD + 2 * NF + NF * b:C_FWD + 2 * NF + NF * (b + 1)] = im
    wre = 2 * np.cos(ang).T / L
    wre[0] = 1.0 / L
    wim = wre.copy()
    wim[0] = alt / L
    wx = -2 * np.sin(ang).T / L
    for b in range(NB):
        for i, w in enumerate((wre, wim, wx)):
            con[NF * b:NF * (b + 1), C_INV + NB * L * i + L * b:C_INV + NB * L * i + L * (b + 1)] = w
    c = np.arange(P)
    con[:, C_REL:C_REL + 8] = (c[:, None] - np.arange(8)) % 8
    con[:, C_HEAD:C_HEAD + J] = c[:, None] // HD == np.arange(J)
    con[:, C_IOTA:C_IOTA + 8] = np.arange(8)
    con[:, C_POW:C_POW + 2] = -0.5
    sel = np.zeros((3, EXPERTS, EXPERTS, P), np.float32)
    for e in range(EXPERTS):
        sel[:, e, e, :] = 1
    return con.astype(np.float32), sel.reshape(3 * EXPERTS, EXPERTS * P)


def kernel(x, ctx_1024, L0_attn_Wqkv, L0_attn_bqkv, L0_attn_Wo, L0_attn_bo, L0_xattn_wq, L0_xattn_wk, L0_xattn_wv,
           L0_xattn_wo, L0_ffn_gate_w, L0_ffn_w_up, L0_ffn_w_down, L0_ffn_expert_bias):
    import numpy as np
    import concourse.bacc as bacc
    from concourse.bass_utils import run_bass_kernel_spmd

    def regroup(w):
        return w.reshape(J, 3, HD, -1).transpose(1, 0, 2, 3).reshape(3 * D, -1)

    wq, wk, wv, wo = (np.asarray(w) for w in (L0_xattn_wq, L0_xattn_wk, L0_xattn_wv, L0_xattn_wo))
    con, sel = constants()
    arrays = {
        "x": np.asarray(x).reshape(B * L, D),
        "ctxt": np.asarray(ctx_1024).reshape(B * L, D),
        "w_qkv": regroup(np.asarray(L0_attn_Wqkv)).T,
        "w_mid": np.concatenate([wk, wv, wo, wq, np.asarray(L0_attn_Wo).T, np.asarray(L0_ffn_gate_w).T], axis=1),
        "w_up": np.asarray(L0_ffn_w_up).transpose(2, 0, 1).reshape(P, EXPERTS * HIDDEN),
        "w_down": np.asarray(L0_ffn_w_down).reshape(EXPERTS, D, 2, P).transpose(3, 0, 2, 1).reshape(P, EXPERTS * 2 * D),
        "rows": np.concatenate([regroup(np.asarray(L0_attn_bqkv)[:, None])[:, 0], np.asarray(L0_attn_bo),
                                np.asarray(L0_ffn_expert_bias)]),
        "consts": con,
        "sel": sel,
    }
    nc = bacc.Bacc("TRN2", target_bir_lowering=False, num_devices=1)
    args = {}
    for name, a in arrays.items():
        arrays[name] = a = np.ascontiguousarray(a)
        args[name] = nc.dram_tensor(name, a.shape, F32, kind="ExternalInput").ap()
    out = nc.dram_tensor("out", (B * L, D), F32, kind="ExternalOutput").ap()
    decoder_layer(nc, out=out, **args)
    got = run_bass_kernel_spmd(nc, [arrays], core_ids=[0])
    return got.results[0]["out"].reshape(B, L, D)
```

```python
from contextlib import ExitStack

import concourse.bass as bass
from concourse import mybir

ALU = mybir.AluOpType
ACT = mybir.ActivationFunctionType
F32 = mybir.dt.float32
BF16 = mybir.dt.bfloat16
U32 = mybir.dt.uint32
F32R = mybir.dt.float32r
AX = mybir.AxisListType

P = 128
D = 128
B, L = 16, 64
TILES = B * L // P
CHUNKS = TILES // 2
J, HD = 16, 8
QUAD = 4
GROUPS = 8
PAIRS = GROUPS // 2
S = 64
NB = 4
NF = 32
TOP = 4
EXPERTS, HIDDEN = 8, 256
EPS = 1e-5
SCALE = float(HD) ** -0.5
HIGH = 0xFFFFF000

W_K, W_V, W_O2, W_Q, W_O, W_GATE = 0, 128, 256, 384, 512, 640
R_BQKV, R_BO, R_EBIAS, R_LEN = 0, 384, 512, 520
C_ID = 0
C_ODD = 128
C_POW = C_ODD + 2
C_FWD = C_POW + 2
C_INV = C_FWD + D
C_REL = C_INV + 3 * NB * L
C_HEAD = C_REL + 8
C_IOTA = C_HEAD + J
C_LEN = C_IOTA + 8


LAYERS = {
    "ctx": {"cdft": 1.28, "cproj": 4.11},
    "self": {"st1": -2.05, "nm1": -0.16, "xt": 1.1, "qkv": 2, "ft": 2.42, "score": 5,
             "exp": 6.47, "flip": 7.47, "vtr": 12.3, "pv": 13.74, "vt2": 15.25, "wo": 16.33},
    "cross": {"st2": 0.01, "nm2": 0.71, "dft": 1.62, "qp": 2, "corr": 3.01, "g": 5, "ov": 6.71, "y2": 7.22},
    "gate": {"st3": 0.25, "nm3": 0.86, "xt3": 1.89, "gate": 2.12, "wt": 3.58, "wb": 4.27},
}
START = {
    "self": (0.7, 6.83, 15.89, 23.44),
    "ctx": (6.38, 9.24, 14.32, 26.98),
    "cross": (20.48, 24.88, 35.77, 42.79),
    "gate": (28.71, 34.84, 42.98, 54.7),
}
PARTS = {"qkv": 2, "ft": 2, "score": QUAD, "exp": QUAD, "flip": QUAD, "vtr": 2, "wb": EXPERTS // 2}
PART_STEP = {"qkv": 0.91, "ft": 1.07, "score": 1.09, "vtr": 1.04, "exp": 1.0, "flip": 0.99, "wb": 1.53}
UNIT = {"up": 0.9, "sq": 1.76, "down": 3.01}
UNIT_START = (32.61, 41.27, 50.99, 61.62)
UNIT_STEP = (0.96, 0.75, 0.81, 0.61)
CHUNK_END = {"acc": 3.68, "fin": 6.2}
WSPLIT = 14.36


def steps():
    found = [(WSPLIT, "wsplit", 0, 0)]
    for a in range(CHUNKS):
        for layer, slots in LAYERS.items():
            for name, slot in slots.items():
                for part in range(PARTS.get(name, 1)):
                    found.append((START[layer][a] + slot + PART_STEP.get(name, 1) * part, name, a, part))
        for e in range(EXPERTS):
            for name, slot in UNIT.items():
                found.append((UNIT_START[a] + UNIT_STEP[a] * e + slot, name, EXPERTS * a + e, 0))
        for name, slot in CHUNK_END.items():
            found.append((UNIT_START[a] + UNIT_STEP[a] * (EXPERTS - 1) + slot, name, a, 0))
    found.sort(key=lambda x: x[0])
    return [x[1:] for x in found]


STEPS = steps()


RING = 7
TURN = ("xt", "cdft", "cproj", "vtr", "vt2", "dft", "g", "ov", "xt3", "gate", "wt", "wb")
WORK = ("qkv", "pv", "wo", "qp", "corr", "y2", "fin")


def numbered(names):
    return {step: n for n, step in enumerate(x for x in STEPS if x[0] in names)}


def decoder_layer(nc, x, ctxt, w_qkv, w_mid, w_up, w_down, rows, consts, sel, idb, out):
    with ExitStack() as ctx:
        def sb(name, shape, dt=F32):
            return ctx.enter_context(nc.sbuf_tensor(name, shape, dt))

        def sem(name):
            return ctx.enter_context(nc.semaphore(name))

        x_sb = sb("x_sb", [P, TILES, D])
        c_sb = sb("c_sb", [P, TILES, D])
        x12 = sb("x12", [P, TILES, D])
        xn = sb("xn", [P, TILES, D])
        stat = sb("stat", [P, 3 * CHUNKS, 2, 6])
        mv = sb("mv", [P, 3 * CHUNKS, 2, 2])
        rstd = sb("rstd", [P, 3 * CHUNKS, 2])
        xt = sb("xt", [P, 2, 2 * P])
        wqkv_sb = sb("wqkv_sb", [P, 3 * D])
        wmid_sb = sb("wmid_sb", [P, W_GATE + EXPERTS])
        wup_sb = sb("wup_sb", [P, EXPERTS, HIDDEN])
        whi = sb("whi", [P, EXPERTS, HIDDEN], F32R)
        wlo = sb("wlo", [P, EXPERTS, HIDDEN], F32R)
        wdn_sb = sb("wdn_sb", [P, EXPERTS, 2, D])
        row_sb = sb("row_sb", [P, R_LEN])
        con = sb("con", [P, C_LEN])
        identb = sb("identb", [P, P], BF16)
        selb = sb("selb", [3 * EXPERTS, EXPERTS, P], BF16)
        nat = sb("nat", [P, 2, 3, J, 32])
        vrow = sb("vrow", [P, 2, D])
        feat = sb("feat", [P, 3, 2, 2, GROUPS, S])
        negm = sb("negm", [P, CHUNKS, QUAD, GROUPS])
        praw = sb("praw", [P, QUAD, GROUPS * S])
        prob = sb("prob", [P, 2, QUAD, PAIRS, P])
        vkey = sb("vkey", [P, 2, 2, PAIRS, P])
        onat = sb("onat", [P, J, 32])
        rden = sb("rden", [P, J, 2])
        vals = sb("vals", [P, 2, 2, D])
        valsT = sb("valsT", [P, 2, 2 * P])
        cx = sb("cx", [P, 2, 4 * P])
        kv = sb("kv", [P, CHUNKS, 4 * P])
        qf = sb("qf", [P, 2, 2 * P])
        prod = sb("prod", [P, 2, 4, D])
        topv = sb("topv", [P, CHUNKS, NB, 8])
        topi = sb("topi", [P, CHUNKS, NB, 8], U32)
        topr = sb("topr", [P, CHUNKS, NB, 8], U32)
        dif = sb("dif", [P, CHUNKS, NB, TOP])
        ex = sb("ex", [P, CHUNKS, NB, TOP])
        exs = sb("exs", [P, CHUNKS, NB])
        exr = sb("exr", [P, CHUNKS, NB])
        wgt = sb("wgt", [P, CHUNKS, NB, TOP])
        hit = sb("hit", [P, NB, 8, TOP])
        w8 = sb("w8", [P, CHUNKS, NB, 8])
        mix = sb("mix", [P, 2, NB, J, 8])
        mixT = sb("mixT", [P, NB, D])
        ovT = sb("ovT", [P, 2, NB, HD, J // 2])
        xn3T = sb("xn3T", [P, 2, 2 * P])
        xtop = sb("xtop", [P, 2, 2 * P], U32)
        xhi = sb("xhi", [P, 2, 2 * P], F32R)
        xlo = sb("xlo", [P, 2, 2 * P], F32R)
        eg = sb("eg", [P, CHUNKS, 2, EXPERTS])
        eg1 = sb("eg1", [P, CHUNKS, 2, EXPERTS])
        gate = sb("gate", [P, CHUNKS, 2, EXPERTS])
        biased = sb("biased", [P, CHUNKS, 2, EXPERTS])
        bestv = sb("bestv", [P, CHUNKS, 2, 8])
        besti = sb("besti", [P, CHUNKS, 2, 8], U32)
        pick = sb("pick", [P, CHUNKS, 2, EXPERTS, 2])
        picked = sb("picked", [P, CHUNKS, 2, EXPERTS])
        wtok = sb("wtok", [P, CHUNKS, 2, EXPERTS])
        rest = sb("rest", [P, CHUNKS, 2, 2, EXPERTS])
        wsplit = sb("wsplit", [P, CHUNKS, 2, 3 * EXPERTS], BF16)
        wT = sb("wT", [3 * EXPERTS, TILES * P], BF16)
        wb_sb = sb("wb_sb", [P, 2, EXPERTS, 2 * P])
        wtop = wb_sb[:, 1].bitcast(U32)
        rel = sb("rel", [P, 2, 4 * P])
        hid = sb("hid", [P, 2, 4 * P])
        accT = sb("accT", [P, 2 * P])
        fin = x_sb

        ps = ctx.enter_context(nc.psum_tensor("ps", [P, 8, 512], F32))
        acc_ps = ps[:, RING, :]
        turn_at, work_at, ring_at = numbered(TURN), numbered(WORK), numbered(TURN + WORK + ("score", "flip", "up"))

        def psum(name, a, part=0):
            return ps[:, ring_at[(name, a, part)] % RING, :]

        ld_x0, ld_x = sem("ld_x0"), sem("ld_x")
        ld_c = sem("ld_c")
        ld_id, ld_con, ld_wqkv, ld_mid, ld_up, ld_dn, ld_row, ld_sel = (
            sem(n) for n in ("ld_id", "ld_con", "ld_wqkv", "ld_mid", "ld_up", "ld_dn", "ld_row", "ld_sel"))
        zeroed = sem("zeroed")
        xb_ready = sem("xb_ready")
        stats_ready = sem("stats_ready")
        agg = sem("agg")
        veps_ready = sem("veps_ready")
        rstd_ready = sem("rstd_ready")
        norm_ready = sem("norm_ready")
        turn_full, turn_free = sem("turn_full"), sem("turn_free")
        work_full, work_free = sem("work_full"), sem("work_free")
        score_full, score_free = sem("score_full"), sem("score_free")
        max_ready = sem("max_ready")
        exp_ready = sem("exp_ready")
        flip_full, flip_free = sem("flip_full"), sem("flip_free")
        vnat_ready = sem("vnat_ready")
        nat_ready = sem("nat_ready")
        bd_ready = sem("bd_ready")
        rden_ready = sem("rden_ready")
        vals_ready = sem("vals_ready")
        prod_ready = sem("prod_ready")
        prodc_ready = sem("prodc_ready")
        top_val = sem("top_val")
        dif_ready = sem("dif_ready")
        ex_ready = sem("ex_ready")
        tk = sem("tk")
        w8_ready = sem("w8_ready")
        mix_ready = sem("mix_ready")
        split_ready = sem("split_ready")
        z_full, z_free = sem("z_full"), sem("z_free")
        hid_ready = sem("hid_ready")
        down_done = sem("down_done")
        acct_ready = sem("acct_ready")
        wtop_ready, whi_ready, wlo_ready = sem("wtop_ready"), sem("whi_ready"), sem("wlo_ready")
        xtop_ready, xhi_ready, xlo_ready = sem("xtop_ready"), sem("xhi_ready"), sem("xlo_ready")
        stored = sem("stored")

        ident = con[:, C_ID:C_ID + P]
        block = ctx.enter_context(nc.Block())

        @block.sync
        def _(sp):
            xv = x.rearrange("(t p) d -> p t d", p=P)
            ov = out.rearrange("(t p) d -> p t d", p=P)
            cv = ctxt.rearrange("(t p) d -> p t d", p=P)
            sp.dma_start(x_sb[:, 0:2, :], xv[:, 0:2, :]).then_inc(ld_x0, 16)
            sp.dma_start(wqkv_sb[:], w_qkv).then_inc(ld_wqkv, 16)
            sp.dma_start(c_sb[:], cv).then_inc(ld_c, 16)
            sp.dma_start(x_sb[:, 2:TILES, :], xv[:, 2:TILES, :]).then_inc(ld_x, 16)
            sp.dma_start(wup_sb[:].rearrange("p e h -> p (e h)"), w_up).then_inc(ld_up, 16)
            sp.dma_start(wdn_sb[:].rearrange("p e c n -> p (e c n)"), w_down).then_inc(ld_dn, 16)
            sp.dma_start(selb[:].rearrange("k e p -> k (e p)"), sel).then_inc(ld_sel, 16)
            sp.dma_start(identb[:], idb).then_inc(ld_sel, 16)
            for name, a, part in STEPS:
                if name == "fin":
                    sp.wait_ge(work_free, work_at[("fin", a, 0)] + 1)
                    sp.dma_start(ov[:, 2 * a:2 * a + 2, :], fin[:, 2 * a:2 * a + 2, :]).then_inc(stored, 16)
            sp.wait_ge(stored, 16 * CHUNKS)

        @block.gpsimd
        def _(pool):
            nc.gpsimd.memset(nat[:], 0.0).then_inc(zeroed, 1)
            pool.wait_ge(zeroed, 1)
            pool.wait_ge(ld_id, 16)
            parity = con[:, C_ODD:C_ODD + 2].unsqueeze(1)
            for t in range(2):
                nc.gpsimd.tensor_copy(nat[:, t, 2, :, 2 * HD:2 * HD + 2], parity.broadcast_to([P, J, 2])).then_inc(zeroed, 1)

            def rsqrt(n):
                pool.wait_ge(stats_ready, 2 * (n + 1))
                if n == 0:
                    pool.wait_ge(ld_id, 16)
                nc.gpsimd.tensor_scalar(rstd[:, n, :], mv[:, n, :, 1], EPS, None, ALU.add).then_inc(veps_ready, 1)
                pool.wait_ge(veps_ready, n + 1)
                nc.gpsimd.tensor_tensor(rstd[:, n, :], rstd[:, n, :], con[:, C_POW:C_POW + 2], ALU.pow).then_inc(rstd_ready, 1)

            norms = 0
            for name, a, part in STEPS:
                if name in ("st1", "st2", "st3"):
                    rsqrt(norms)
                    norms += 1
                if name == "qkv":
                    t = part
                    pool.wait_ge(work_free, work_at[("qkv", a, t)] + 1)
                    if a:
                        pool.wait_ge(bd_ready, 6 * (a - 1) + 3 * (t + 1))
                    nc.gpsimd.tensor_tensor(
                        nat[:, t, 2, :, 0:2 * HD].rearrange("p j (g d) -> p j g d", d=HD),
                        vrow[:, t].rearrange("p (j d) -> p j d", d=HD).unsqueeze(2).broadcast_to([P, J, 2, HD]),
                        parity.unsqueeze(3).broadcast_to([P, J, 2, HD]), ALU.mult).then_inc(vnat_ready, 1)
                if name == "vtr" and part == 0 and a == 0:
                    pool.wait_ge(ld_row, 16)
                    pool.wait_ge(ld_x, 16)
                    nc.gpsimd.tensor_tensor(x12[:], x_sb[:], row_sb[:, R_BO:R_BO + D].unsqueeze(1).broadcast_to([P, TILES, D]),
                                            ALU.add).then_inc(xb_ready, 1)
                if name == "wsplit":
                    pool.wait_ge(wtop_ready, 1)
                    nc.gpsimd.tensor_tensor(wlo[:], wup_sb[:], wtop.bitcast(F32), ALU.subtract).then_inc(wlo_ready, 1)
                if name == "xt3":
                    pool.wait_ge(xtop_ready, a + 1)
                    if a >= 2:
                        pool.wait_ge(z_full, EXPERTS * (a - 1))
                    nc.gpsimd.tensor_copy(xhi[:, a % 2, :], xtop[:, a % 2, :].bitcast(F32)).then_inc(xhi_ready, 1)
                    nc.gpsimd.tensor_tensor(xlo[:, a % 2, :], xn3T[:, a % 2, :], xtop[:, a % 2, :].bitcast(F32),
                                            ALU.subtract).then_inc(xlo_ready, 1)
                if name == "corr":
                    pool.wait_ge(w8_ready, a + 1)
                    if a >= 2:
                        pool.wait_ge(turn_full, turn_at[("g", a - 2, 0)] + 1)
                    for b in range(NB):
                        last = nc.gpsimd.tensor_tensor(
                            mix[:, a % 2, b], w8[:, a, b, :].unsqueeze(1).broadcast_to([P, J, 8]),
                            con[:, C_HEAD:C_HEAD + J].unsqueeze(2).broadcast_to([P, J, 8]), ALU.mult)
                    last.then_inc(mix_ready, 1)

        @block.scalar
        def _(act):
            act.dma_start(con[:, 0:C_FWD], consts[:, 0:C_FWD]).then_inc(ld_id, 16)
            act.dma_start(row_sb[:], rows.partition_broadcast(P)).then_inc(ld_row, 16)
            act.dma_start(con[:, C_FWD:C_LEN], consts[:, C_FWD:C_LEN]).then_inc(ld_con, 16)
            act.dma_start(wmid_sb[:], w_mid).then_inc(ld_mid, 16)

            def turn(step, dst, src):
                act.wait_ge(turn_full, turn_at[step] + 1)
                nc.scalar.copy(dst, src).then_inc(turn_free, 1)

            for step in STEPS:
                name, a, part = step
                turn_ps = psum(*step) if name in TURN else None
                if name == "xt":
                    if a >= 2:
                        act.wait_ge(work_full, work_at[("qkv", a - 2, 1)] + 1)
                    turn(step, xt[:, a % 2, :], turn_ps[:, 0:2 * P])
                if name == "cdft":
                    if a >= 2:
                        act.wait_ge(turn_full, turn_at[("cproj", a - 2, 0)] + 1)
                    turn(step, cx[:, a % 2, :], turn_ps)
                if name == "cproj":
                    turn(step, kv[:, a, :], turn_ps)
                if name == "vtr":
                    if a >= 2:
                        act.wait_ge(work_full, work_at[("pv", a - 2, 0)] + 1)
                    turn(step, vkey[:, a % 2, part], turn_ps.rearrange("p (i n) -> p i n", n=P))
                if name == "exp":
                    act.wait_ge(score_free, QUAD * a + part + 1)
                    nc.scalar.activation(praw[:, part], praw[:, part], ACT.Exp, scale=SCALE).then_inc(exp_ready, 1)
                if name == "flip":
                    act.wait_ge(flip_full, QUAD * a + part + 1)
                    if a >= 2:
                        act.wait_ge(work_full, work_at[("pv", a - 2, 0)] + 1)
                    nc.scalar.copy(prob[:, a % 2, part], psum(*step).rearrange("p (i n) -> p i n", n=P)).then_inc(flip_free, 1)
                if name == "vt2":
                    if a >= 2:
                        act.wait_ge(work_full, work_at[("wo", a - 2, 0)] + 1)
                    act.wait_ge(turn_full, turn_at[step] + 1)
                    for t in range(2):
                        for g in range(2):
                            last = nc.scalar.copy(
                                valsT[:, a % 2, P * t:P * (t + 1)].rearrange("p (c g r) -> p c g r", g=2, r=4)[:, :, g],
                                turn_ps[:, P * g:P * (g + 1)].rearrange("p (q t c) -> p t q c", q=QUAD, t=2)[:, t].rearrange(
                                    "p q (i r) -> p q i r", r=4))
                    last.then_inc(turn_free, 1)
                if name == "dft":
                    if a >= 2:
                        act.wait_ge(work_full, work_at[("qp", a - 2, 0)] + 1)
                    turn(step, qf[:, a % 2, :], turn_ps[:, 0:2 * P])
                if name == "corr":
                    act.wait_ge(dif_ready, a + 1)
                    nc.scalar.activation(ex[:, a], dif[:, a], ACT.Exp).then_inc(ex_ready, 1)
                if name == "g":
                    if a >= 1:
                        act.wait_ge(turn_full, turn_at[("ov", a - 1, 0)] + 1)
                    turn(step, mixT[:], turn_ps.rearrange("p (b n) -> p b n", n=D))
                if name == "ov":
                    if a >= 2:
                        act.wait_ge(work_full, work_at[("y2", a - 2, 0)] + 1)
                    turn(step, ovT[:, a % 2].rearrange("p b d h -> p b h d"),
                         turn_ps[:, 0:NB * L].rearrange("p (b h d) -> p b h d", b=NB, d=HD))
                if name == "xt3":
                    if a >= 2:
                        act.wait_ge(turn_full, turn_at[("gate", a - 2, 0)] + 1)
                        act.wait_ge(xlo_ready, a - 1)
                    turn(step, xn3T[:, a % 2, :], turn_ps[:, 0:2 * P])
                if name == "gate":
                    act.wait_ge(turn_full, turn_at[step] + 1)
                    nc.scalar.activation(eg[:, a].rearrange("p t e -> p (t e)"), turn_ps[:, 0:2 * EXPERTS], ACT.Exp,
                                         scale=-1.0).then_inc(turn_free, 1)
                if name == "wt":
                    turn(step, wT[:, 2 * P * a:2 * P * (a + 1)], turn_ps.bitcast(BF16)[0:3 * EXPERTS, 0:2 * P])
                if name == "wsplit":
                    act.wait_ge(wtop_ready, 1)
                    nc.scalar.copy(whi[:], wtop.bitcast(F32)).then_inc(whi_ready, 1)
                if name == "wb":
                    if a == 1:
                        act.wait_ge(whi_ready, 1)
                        act.wait_ge(wlo_ready, 1)
                    if a >= 2:
                        act.wait_ge(z_free, EXPERTS * (a - 2) + 2 * part + 2)
                    turn(step, wb_sb[:, a % 2, 2 * part:2 * part + 2, :], turn_ps.rearrange("p (e t) -> p e t", e=2))
                if name == "sq":
                    act.wait_ge(z_free, a + 1)
                    if a >= 2:
                        act.wait_ge(down_done, a - 1)
                    nc.scalar.activation(hid[:, a % 2, :], rel[:, a % 2, :], ACT.Square).then_inc(hid_ready, 1)
                if name == "acc":
                    act.wait_ge(down_done, EXPERTS * (a + 1))
                    if a:
                        act.wait_ge(work_full, work_at[("fin", a - 1, 0)] + 1)
                    nc.scalar.copy(accT[:], acc_ps[:, 0:2 * P]).then_inc(acct_ready, 1)

        @block.vector
        def _(dve):
            chain = [0]

            def link(ins):
                chain[0] += 1
                ins.then_inc(tk, 1)
                dve.wait_ge(tk, chain[0])

            def stats(n, src, a):
                for t in range(2):
                    nc.vector.bn_stats(stat[:, n, t, :], src[:, 2 * a + t, :]).then_inc(agg, 1)
                for t in range(2):
                    dve.wait_ge(agg, 2 * n + t + 1)
                    nc.vector.bn_aggr(mv[:, n, t, :], stat[:, n, t, :]).then_inc(stats_ready, 1)

            def normalise(n, dst, src, a):
                dve.wait_ge(rstd_ready, n + 1)
                dve.wait_ge(stats_ready, 2 * (n + 1))
                for t in range(2):
                    nc.vector.tensor_scalar(dst[:, 2 * a + t, :], src[:, 2 * a + t, :], mv[:, n, t, 0:1], rstd[:, n, t:t + 1],
                                            ALU.subtract, ALU.mult).then_inc(norm_ready, 1)

            def work(name, a, part=0):
                use = work_at[(name, a, part)]
                dve.wait_ge(work_full, use + 1)
                return psum(name, a, part)

            norm_no = {}
            for name, a, part in STEPS:
                if name in ("st1", "st2", "st3"):
                    if name == "st1":
                        dve.wait_ge(ld_x if a else ld_x0, 16)
                    norm_no[(name[2], a)] = len(norm_no)
                    stats(norm_no[(name[2], a)], {"1": x_sb, "2": x12, "3": x12}[name[2]], a)
                if name == "nm1":
                    normalise(norm_no[("1", a)], xn, x_sb, a)
                if name == "qkv":
                    t = part
                    if a == 0:
                        dve.wait_ge(zeroed, 3)
                        dve.wait_ge(ld_row, 16)
                    if a > 0:
                        dve.wait_ge(bd_ready, 6 * (a - 1) + 3 * (t + 1))
                    bias = row_sb[:, R_BQKV:R_BQKV + 3 * D].rearrange("p (c d) -> p c d", d=HD)
                    proj = work(name, a, t)[:, 0:3 * D].rearrange("p (c d) -> p c d", d=HD)
                    nc.vector.tensor_tensor(nat[:, t, 0:2, :, 0:HD].rearrange("p c j d -> p (c j) d"),
                                            proj[:, 0:2 * J], bias[:, 0:2 * J], ALU.add).then_inc(nat_ready, 1)
                    if a > 0:
                        dve.wait_ge(vnat_ready, 2 * (a - 1) + t + 1)
                    nc.vector.tensor_tensor(vrow[:, t].rearrange("p (j d) -> p j d", d=HD), proj[:, 2 * J:3 * J],
                                            bias[:, 2 * J:3 * J], ALU.add).then_inc(work_free, 1)
                if name == "ft":
                    t = part
                    dve.wait_ge(nat_ready, 2 * a + t + 1)
                    if a >= 2:
                        dve.wait_ge(score_full, QUAD * (a - 1))
                        dve.wait_ge(turn_full, turn_at[("vtr", a - 2, 1)] + 1)
                    for c in range(3):
                        if c == 2:
                            dve.wait_ge(vnat_ready, 2 * a + t + 1)
                        nc.vector.transpose(feat[:, c, a % 2, t].rearrange("p h (j r) -> p j h r", j=J),
                                            nat[:, t, c, :, :]).then_inc(bd_ready, 1)
                if name == "score":
                    dve.wait_ge(score_full, QUAD * a + part + 1)
                    if a:
                        dve.wait_ge(flip_full, QUAD * (a - 1) + part + 1)
                    s_ps = psum(name, a, part).rearrange("p (h s) -> p h s", s=S)
                    nc.vector.tensor_reduce(negm[:, a, part, :], s_ps, AX.X, ALU.max, negate=True).then_inc(max_ready, 1)
                    dve.wait_ge(max_ready, QUAD * a + part + 1)
                    nc.vector.tensor_tensor(praw[:, part].rearrange("p (h s) -> p h s", s=S), s_ps,
                                            negm[:, a, part, :].unsqueeze(2).broadcast_to([P, GROUPS, S]),
                                            ALU.add).then_inc(score_free, 1)
                if name == "pv":
                    if a:
                        dve.wait_ge(vals_ready, 2 * a)
                    nc.vector.transpose(onat[:], work(name, a).rearrange("p (h j r) -> p j h r", h=GROUPS, j=J)).then_inc(work_free, 1)
                    dve.wait_ge(work_free, work_at[(name, a, 0)] + 1)
                    nc.vector.reciprocal(rden[:], onat[:, :, 2 * HD:2 * HD + 2]).then_inc(rden_ready, 1)
                    dve.wait_ge(rden_ready, a + 1)
                    if a >= 2:
                        dve.wait_ge(turn_full, turn_at[("vt2", a - 2, 0)] + 1)
                    for g in range(2):
                        nc.vector.tensor_tensor(
                            vals[:, a % 2, g].rearrange("p (j d) -> p j d", d=HD), onat[:, :, HD * g:HD * (g + 1)],
                            rden[:, :, g:g + 1].broadcast_to([P, J, HD]), ALU.mult).then_inc(vals_ready, 1)
                if name == "wo":
                    if a == 0:
                        dve.wait_ge(xb_ready, 1)
                    both = x12[:, 2 * a:2 * a + 2, :]
                    nc.vector.tensor_tensor(both, work(name, a)[:, 0:2 * D].rearrange("p (t n) -> p t n", n=D), both,
                                            ALU.add).then_inc(work_free, 1)
                    dve.wait_ge(work_free, work_at[(name, a, 0)] + 1)
                if name == "nm2":
                    dve.wait_ge(turn_full, turn_at[("xt", a, 0)] + 1)
                    normalise(norm_no[("2", a)], xn, x12, a)
                if name == "qp":
                    if a >= 2:
                        dve.wait_ge(work_full, work_at[("corr", a - 2, 0)] + 1)
                    dve.wait_ge(turn_free, turn_at[("cproj", a, 0)] + 1)
                    spec = work(name, a)
                    nc.vector.tensor_tensor(prod[:, a % 2, 0:2, :], spec[:, 0:2 * D].rearrange("p (i c) -> p i c", c=D),
                                            kv[:, a, 0:2 * D].rearrange("p (i c) -> p i c", c=D), ALU.mult).then_inc(prod_ready, 1)
                    nc.vector.tensor_tensor(prod[:, a % 2, 3, :], spec[:, 0:D], kv[:, a, D:2 * D], ALU.mult).then_inc(prodc_ready, 1)
                    nc.vector.tensor_tensor(prod[:, a % 2, 2, :], spec[:, D:2 * D], kv[:, a, 0:D], ALU.mult).then_inc(work_free, 1)
                    dve.wait_ge(prodc_ready, 2 * a + 1)
                    dve.wait_ge(work_free, work_at[(name, a, 0)] + 1)
                    nc.vector.tensor_tensor(prod[:, a % 2, 2, :], prod[:, a % 2, 2, :], prod[:, a % 2, 3, :],
                                            ALU.subtract).then_inc(prodc_ready, 1)
                if name == "corr":
                    corr = work(name, a)[:, 0:NB * L].rearrange("p (b s) -> p b s", s=L)
                    for b in range(NB):
                        nc.vector.max(topv[:, a, b, :], corr[:, b, :]).then_inc(top_val, 1)
                    for b in range(NB):
                        dve.wait_ge(top_val, NB * a + b + 1)
                        last = nc.vector.max_index(topi[:, a, b, :], topv[:, a, b, :], corr[:, b, :])
                    last.then_inc(work_free, 1)
                    dve.wait_ge(work_free, work_at[(name, a, 0)] + 1)
                    nc.vector.tensor_tensor(dif[:, a], topv[:, a, :, 0:TOP], topv[:, a, :, 0:1].broadcast_to([P, NB, TOP]),
                                            ALU.subtract).then_inc(dif_ready, 1)
                    if a:
                        dve.wait_ge(w8_ready, a)
                    link(nc.vector.tensor_single_scalar(topr[:, a], topi[:, a], HD - 1, ALU.bitwise_and))
                    if a == 0:
                        dve.wait_ge(ld_con, 16)
                    for b in range(NB):
                        last = nc.vector.tensor_tensor(
                            hit[:, b], topr[:, a, b, 0:TOP].unsqueeze(1).broadcast_to([P, 8, TOP]),
                            con[:, C_REL:C_REL + 8].unsqueeze(2).broadcast_to([P, 8, TOP]), ALU.is_equal)
                        if b < NB - 1:
                            link(last)
                    link(last)
                    dve.wait_ge(ex_ready, a + 1)
                    link(nc.vector.tensor_reduce(exs[:, a], ex[:, a], AX.X, ALU.add))
                    link(nc.vector.reciprocal(exr[:, a], exs[:, a]))
                    link(nc.vector.tensor_tensor(wgt[:, a], ex[:, a], exr[:, a].unsqueeze(2).broadcast_to([P, NB, TOP]), ALU.mult))
                    link(nc.vector.tensor_tensor(hit[:], hit[:], wgt[:, a].unsqueeze(2).broadcast_to([P, NB, 8, TOP]), ALU.mult))
                    nc.vector.tensor_reduce(w8[:, a], hit[:], AX.X, ALU.add).then_inc(w8_ready, 1)
                if name == "y2":
                    dve.wait_ge(work_free, work_at[("wo", a, 0)] + 1)
                    nc.vector.tensor_tensor(x12[:, 2 * a:2 * a + 2, :], work(name, a)[:, 0:2 * D].rearrange("p (t n) -> p t n", n=D),
                                            x12[:, 2 * a:2 * a + 2, :], ALU.add).then_inc(work_free, 1)
                    dve.wait_ge(work_free, work_at[(name, a, 0)] + 1)
                if name == "nm3":
                    dve.wait_ge(turn_full, turn_at[("dft", a, 0)] + 1)
                    normalise(norm_no[("3", a)], xn, x12, a)
                if name == "xt3":
                    dve.wait_ge(turn_free, turn_at[(name, a, 0)] + 1)
                    if a >= 2:
                        dve.wait_ge(xhi_ready, a - 1)
                        dve.wait_ge(xlo_ready, a - 1)
                    nc.vector.tensor_single_scalar(xtop[:, a % 2, :], xn3T[:, a % 2, :].bitcast(U32), HIGH,
                                                   ALU.bitwise_and).then_inc(xtop_ready, 1)
                if name == "wsplit":
                    dve.wait_ge(ld_up, 16)
                    nc.vector.tensor_single_scalar(wtop, wup_sb[:].bitcast(U32), HIGH, ALU.bitwise_and).then_inc(wtop_ready, 1)
                if name == "gate":
                    dve.wait_ge(turn_free, turn_at[(name, a, 0)] + 1)
                    link(nc.vector.tensor_scalar(eg1[:, a], eg[:, a], 1.0, None, ALU.add))
                    link(nc.vector.reciprocal(gate[:, a], eg1[:, a]))
                    link(nc.vector.tensor_tensor(biased[:, a], gate[:, a],
                                                 row_sb[:, R_EBIAS:R_EBIAS + EXPERTS].unsqueeze(1).broadcast_to([P, 2, EXPERTS]), ALU.add))
                    for t in range(2):
                        link(nc.vector.max(bestv[:, a, t], biased[:, a, t]))
                        link(nc.vector.max_index(besti[:, a, t], bestv[:, a, t], biased[:, a, t]))
                    for t in range(2):
                        link(nc.vector.tensor_tensor(pick[:, a, t], besti[:, a, t, 0:2].unsqueeze(1).broadcast_to([P, EXPERTS, 2]),
                                                     con[:, C_IOTA:C_IOTA + 8].unsqueeze(2).broadcast_to([P, EXPERTS, 2]), ALU.is_equal))
                    link(nc.vector.tensor_reduce(picked[:, a], pick[:, a], AX.X, ALU.add))
                    link(nc.vector.tensor_tensor(wtok[:, a], picked[:, a], gate[:, a], ALU.mult))
                    part = [wsplit[:, a, :, EXPERTS * i:EXPERTS * (i + 1)] for i in range(3)]
                    link(nc.vector.tensor_copy(part[0], wtok[:, a]))
                    link(nc.vector.tensor_tensor(rest[:, a, 0], wtok[:, a], part[0], ALU.subtract))
                    link(nc.vector.tensor_copy(part[1], rest[:, a, 0]))
                    link(nc.vector.tensor_tensor(rest[:, a, 1], rest[:, a, 0], part[1], ALU.subtract))
                    nc.vector.tensor_copy(part[2], rest[:, a, 1]).then_inc(split_ready, 1)
                if name == "up":
                    c, e = divmod(a, EXPERTS)
                    dve.wait_ge(turn_free, turn_at[("wb", c, e // 2)] + 1)
                    dve.wait_ge(z_full, a + 1)
                    if a >= 2:
                        dve.wait_ge(hid_ready, a - 1)
                    w_bc = wb_sb[:, (a // EXPERTS) % 2, a % EXPERTS, :].unsqueeze(1).broadcast_to([P, 2, 2 * P])
                    nc.vector.scalar_tensor_tensor(rel[:, a % 2, :].rearrange("p (c t) -> p c t", c=2),
                                                   psum(name, a).rearrange("p (c t) -> p c t", c=2), 0.0, w_bc, ALU.max,
                                                   ALU.mult).then_inc(z_free, 1)
                if name == "fin":
                    nc.vector.tensor_tensor(fin[:, 2 * a:2 * a + 2, :], work(name, a)[:, 0:2 * P].rearrange("p (t n) -> p t n", n=D),
                                            x12[:, 2 * a:2 * a + 2, :], ALU.add).then_inc(work_free, 1)

        @block.tensor
        def _(pe):
            def bank(name, a, part=0):
                use = ring_at[(name, a, part)]
                if use >= RING:
                    last = ring_order[use - RING]
                    was, c, r = last
                    if was in TURN:
                        pe.wait_ge(turn_free, turn_at[last] + 1)
                    elif was in WORK:
                        pe.wait_ge(work_free, work_at[last] + 1)
                    elif was == "score":
                        pe.wait_ge(score_free, QUAD * c + r + 1)
                    elif was == "flip":
                        pe.wait_ge(flip_free, QUAD * c + r + 1)
                    else:
                        pe.wait_ge(z_free, c + 1)
                return psum(name, a, part)

            def turned(name, a):
                pe.wait_ge(turn_free, turn_at[(name, a, 0)] + 1)

            mm = nc.tensor.matmul
            ring_order = list(ring_at)
            norm_no = {}

            for name, a, part in STEPS:
                if name in ("nm1", "nm2", "nm3"):
                    norm_no[(name, a)] = len(norm_no) + 1
                if name in ("xt", "xt3"):
                    if name == "xt" and a == 0:
                        pe.wait_ge(ld_id, 16)
                    pe.wait_ge(norm_ready, 2 * norm_no[("nm1" if name == "xt" else "nm3", a)])
                    ps_t = bank(name, a)
                    for t in range(2):
                        last = nc.tensor.transpose(ps_t[:, P * t:P * (t + 1)], xn[:, 2 * a + t, :], ident)
                    last.then_inc(turn_full, 1)
                if name == "qkv":
                    if a == 0:
                        pe.wait_ge(ld_wqkv, 16)
                    turned("xt", a)
                    mm(bank(name, a, part)[:, 0:3 * D], xt[:, a % 2, P * part:P * (part + 1)], wqkv_sb[:], start=True,
                       stop=True).then_inc(work_full, 1)
                if name == "cdft":
                    if a == 0:
                        pe.wait_ge(ld_id, 16)
                        pe.wait_ge(ld_c, 16)
                        pe.wait_ge(ld_con, 16)
                    ps_t = bank(name, a)
                    spec = ps_t[:, 0:2 * P].rearrange("p (i t f) -> p i t f", i=2, t=2)
                    for t in range(2):
                        mm(spec[:, :, t, :], c_sb[:, 2 * a + t, :], con[:, C_FWD:C_FWD + 2 * 2 * NF].rearrange("p (i f) -> p i f", i=2),
                           start=True, stop=True)
                        last = nc.tensor.transpose(ps_t[:, 2 * P + P * t:2 * P + P * (t + 1)], c_sb[:, 2 * a + t, :], ident)
                    last.then_inc(turn_full, 1)
                if name == "cproj":
                    if a == 0:
                        pe.wait_ge(ld_mid, 16)
                    turned("cdft", a)
                    ps_s = bank(name, a)
                    for i in range(2):
                        mm(ps_s[:, D * i:D * (i + 1)], cx[:, a % 2, P * i:P * (i + 1)], wmid_sb[:, W_K:W_K + D], start=True, stop=True)
                    mm(ps_s[:, 2 * P:4 * P], wmid_sb[:, W_V:W_V + D], cx[:, a % 2, 2 * P:4 * P], start=True,
                       stop=True).then_inc(turn_full, 1)
                if name == "score":
                    if part == 0:
                        pe.wait_ge(bd_ready, 6 * (a + 1))
                    s_ps, q = bank(name, a, part), 32 * part
                    for h in range(GROUPS):
                        for g in range(2):
                            cols = slice(S * g, S * (g + 1))
                            last = mm(s_ps[cols, S * h:S * (h + 1)], feat[q:q + HD, 0, a % 2, g, h, :],
                                      feat[q:q + HD, 1, a % 2, g, h, :], start=True, stop=True)
                    last.then_inc(score_full, 1)
                if name == "flip":
                    pe.wait_ge(exp_ready, QUAD * a + part + 1)
                    t_ps = bank(name, a, part)
                    for i in range(PAIRS):
                        last = nc.tensor.transpose(t_ps[:, P * i:P * (i + 1)], praw[:, part, P * i:P * (i + 1)], ident)
                    last.then_inc(flip_full, 1)
                if name == "vtr":
                    if part == 0:
                        pe.wait_ge(bd_ready, 6 * (a + 1))
                    ps_s = bank(name, a, part)
                    for i in range(PAIRS):
                        last = nc.tensor.transpose(ps_s[:, P * i:P * (i + 1)],
                                                   feat[:, 2, a % 2, part, 2 * i:2 * i + 2, :].rearrange("p h s -> p (h s)"), ident)
                    last.then_inc(turn_full, 1)
                if name == "pv":
                    pe.wait_ge(turn_free, turn_at[("vtr", a, 1)] + 1)
                    o_ps = bank(name, a)
                    for r in range(QUAD):
                        pe.wait_ge(flip_free, QUAD * a + r + 1)
                        for t in range(2):
                            for i in range(PAIRS):
                                last = mm(o_ps[32 * r:32 * r + 32, S * (PAIRS * t + i):S * (PAIRS * t + i + 1)],
                                          vkey[:, a % 2, t, i, 32 * r:32 * r + 32], prob[:, a % 2, r, i, S * t:S * (t + 1)],
                                          start=True, stop=True)
                    last.then_inc(work_full, 1)
                if name == "vt2":
                    pe.wait_ge(vals_ready, 2 * (a + 1))
                    ps_t = bank(name, a)
                    for t in range(2):
                        last = nc.tensor.transpose(ps_t[:, P * t:P * (t + 1)], vals[:, a % 2, t, :], ident)
                    last.then_inc(turn_full, 1)
                if name == "wo":
                    turned("vt2", a)
                    y_ps = bank(name, a)
                    for t in range(2):
                        last = mm(y_ps[:, D * t:D * (t + 1)], valsT[:, a % 2, P * t:P * (t + 1)], wmid_sb[:, W_O:W_O + D],
                                  start=True, stop=True)
                    last.then_inc(work_full, 1)
                if name == "dft":
                    pe.wait_ge(norm_ready, 2 * norm_no[("nm2", a)])
                    ps_t = bank(name, a)
                    spec = ps_t[:, 0:2 * P].rearrange("p (i t f) -> p i t f", i=2, t=2)
                    for t in range(2):
                        last = mm(spec[:, :, t, :], xn[:, 2 * a + t, :],
                                  con[:, C_FWD:C_FWD + 2 * 2 * NF].rearrange("p (i f) -> p i f", i=2), start=True, stop=True)
                    last.then_inc(turn_full, 1)
                if name == "qp":
                    turned("dft", a)
                    q_ps = bank(name, a)
                    for i in range(2):
                        last = mm(q_ps[:, D * i:D * (i + 1)], qf[:, a % 2, P * i:P * (i + 1)], wmid_sb[:, W_Q:W_Q + D],
                                  start=True, stop=True)
                    last.then_inc(work_full, 1)
                if name == "corr":
                    pe.wait_ge(prod_ready, a + 1)
                    pe.wait_ge(prodc_ready, 2 * (a + 1))
                    c_ps = bank(name, a)
                    for i in range(3):
                        last = mm(c_ps[:, 0:NB * L], prod[:, a % 2, i, :], con[:, C_INV + NB * L * i:C_INV + NB * L * (i + 1)],
                                  start=(i == 0), stop=(i == 2))
                    last.then_inc(work_full, 1)
                if name == "g":
                    pe.wait_ge(mix_ready, a + 1)
                    ps_t = bank(name, a)
                    for b in range(NB):
                        last = nc.tensor.transpose(ps_t[:, D * b:D * (b + 1)], mix[:, a % 2, b].rearrange("p h e -> p (h e)"), ident)
                    last.then_inc(turn_full, 1)
                if name == "ov":
                    turned("g", a)
                    ps_t = bank(name, a)
                    for b in range(NB):
                        for odd in range(2):
                            last = mm(ps_t[L * odd:L * (odd + 1), L * b:L * (b + 1)], kv[:, a, 2 * P + L * b:2 * P + L * (b + 1)],
                                      mixT[:, b, :].rearrange("p (h o d) -> p o h d", o=2, d=HD)[:, odd], start=True, stop=True)
                    last.then_inc(turn_full, 1)
                if name == "y2":
                    turned("ov", a)
                    y_ps = bank(name, a)
                    for t in range(2):
                        last = mm(y_ps[:, D * t:D * (t + 1)], ovT[:, a % 2, 2 * t:2 * t + 2].rearrange("p b d h -> p (b d h)"),
                                  wmid_sb[:, W_O2:W_O2 + D], start=True, stop=True)
                    last.then_inc(work_full, 1)
                if name == "gate":
                    turned("xt3", a)
                    ps_t = bank(name, a)
                    for t in range(2):
                        last = mm(ps_t[:, EXPERTS * t:EXPERTS * (t + 1)], xn3T[:, a % 2, P * t:P * (t + 1)],
                                  wmid_sb[:, W_GATE:W_GATE + EXPERTS], start=True, stop=True)
                    last.then_inc(turn_full, 1)
                if name == "wt":
                    pe.wait_ge(split_ready, a + 1)
                    ps_t = bank(name, a).bitcast(BF16)
                    if a == 0:
                        pe.wait_ge(ld_sel, 32)
                    for t in range(2):
                        last = nc.tensor.transpose(ps_t[0:3 * EXPERTS, P * t:P * (t + 1)], wsplit[:, a, t, :], identb[:])
                    last.then_inc(turn_full, 1)
                if name == "wb":
                    turned("wt", a)
                    ps_t = bank(name, a, part)
                    for i in range(2):
                        last = mm(ps_t[:, 2 * P * i:2 * P * (i + 1)], selb[:, 2 * part + i, :], wT[:, 2 * P * a:2 * P * (a + 1)],
                                  start=True, stop=True)
                    last.then_inc(turn_full, 1)
                if name == "up":
                    c, e = divmod(a, EXPERTS)
                    if e == 0:
                        pe.wait_ge(xhi_ready, c + 1)
                        pe.wait_ge(xlo_ready, c + 1)
                    if a == 0:
                        pe.wait_ge(whi_ready, 1)
                        pe.wait_ge(wlo_ready, 1)
                    z_ps = bank(name, a)
                    for half in range(2):
                        for i, (w, r) in enumerate(((whi, xhi), (whi, xlo), (wlo, xhi))):
                            last = mm(z_ps[:, 2 * P * half:2 * P * (half + 1)], w[:, e, P * half:P * (half + 1)], r[:, c % 2, :],
                                      start=(i == 0), stop=(i == 2))
                    last.then_inc(z_full, 1)
                if name == "down":
                    c, e = divmod(a, EXPERTS)
                    if a == 0:
                        pe.wait_ge(ld_dn, 16)
                    if c and e == 0:
                        pe.wait_ge(acct_ready, c)
                    pe.wait_ge(hid_ready, a + 1)
                    for half in range(2):
                        last = mm(acc_ps[:, 0:2 * P], wdn_sb[:, e, half, :], hid[:, a % 2, 2 * P * half:2 * P * (half + 1)],
                                  start=(e == 0 and half == 0), stop=(e == EXPERTS - 1 and half == 1))
                    last.then_inc(down_done, 1)
                if name == "fin":
                    pe.wait_ge(acct_ready, a + 1)
                    f_ps = bank(name, a)
                    for t in range(2):
                        last = nc.tensor.transpose(f_ps[:, P * t:P * (t + 1)], accT[:, P * t:P * (t + 1)], ident)
                    last.then_inc(work_full, 1)


def constants():
    import numpy as np
    con = np.zeros((P, C_LEN), np.float64)
    con[:, C_ID:C_ID + P] = np.eye(P)
    con[:, C_ODD] = np.arange(P) // 4 % 2 == 0
    con[:, C_ODD + 1] = np.arange(P) // 4 % 2 == 1
    l, f = np.arange(L), np.arange(NF)
    ang = 2 * np.pi * np.outer(l, f) / L
    alt = np.where(l % 2 == 0, 1.0, -1.0)
    re, im = np.cos(ang), -np.sin(ang)
    im[:, 0] = alt
    for b in range(2):
        con[L * b:L * (b + 1), C_FWD + NF * b:C_FWD + NF * (b + 1)] = re
        con[L * b:L * (b + 1), C_FWD + 2 * NF + NF * b:C_FWD + 2 * NF + NF * (b + 1)] = im
    wre = 2 * np.cos(ang).T / L
    wre[0] = 1.0 / L
    wim = wre.copy()
    wim[0] = alt / L
    wx = -2 * np.sin(ang).T / L
    for b in range(NB):
        for i, w in enumerate((wre, wim, wx)):
            con[NF * b:NF * (b + 1), C_INV + NB * L * i + L * b:C_INV + NB * L * i + L * (b + 1)] = w
    c = np.arange(P)
    con[:, C_REL:C_REL + 8] = (c[:, None] - np.arange(8)) % 8
    con[:, C_HEAD:C_HEAD + J] = c[:, None] // HD == np.arange(J)
    con[:, C_IOTA:C_IOTA + 8] = np.arange(8)
    con[:, C_POW:C_POW + 2] = -0.5
    sel = np.zeros((3, EXPERTS, EXPERTS, P), np.float32)
    for e in range(EXPERTS):
        sel[:, e, e, :] = 1
    return con.astype(np.float32), sel.reshape(3 * EXPERTS, EXPERTS * P).astype(np.dtype("bfloat16"))


def kernel(x, ctx_1024, L0_attn_Wqkv, L0_attn_bqkv, L0_attn_Wo, L0_attn_bo, L0_xattn_wq, L0_xattn_wk, L0_xattn_wv,
           L0_xattn_wo, L0_ffn_gate_w, L0_ffn_w_up, L0_ffn_w_down, L0_ffn_expert_bias):
    import numpy as np
    import concourse.bacc as bacc
    from concourse.bass_utils import run_bass_kernel_spmd

    def regroup(w):
        return w.reshape(J, 3, HD, -1).transpose(1, 0, 2, 3).reshape(3 * D, -1)

    wq, wk, wv, wo = (np.asarray(w) for w in (L0_xattn_wq, L0_xattn_wk, L0_xattn_wv, L0_xattn_wo))
    con, sel = constants()
    arrays = {
        "x": np.asarray(x).reshape(B * L, D),
        "ctxt": np.asarray(ctx_1024).reshape(B * L, D),
        "w_qkv": regroup(np.asarray(L0_attn_Wqkv)).T,
        "w_mid": np.concatenate([wk, wv, wo, wq, np.asarray(L0_attn_Wo).T, np.asarray(L0_ffn_gate_w).T], axis=1),
        "w_up": np.asarray(L0_ffn_w_up).transpose(2, 0, 1).reshape(P, EXPERTS * HIDDEN),
        "w_down": np.asarray(L0_ffn_w_down).reshape(EXPERTS, D, 2, P).transpose(3, 0, 2, 1).reshape(P, EXPERTS * 2 * D),
        "rows": np.concatenate([regroup(np.asarray(L0_attn_bqkv)[:, None])[:, 0], np.asarray(L0_attn_bo),
                                np.asarray(L0_ffn_expert_bias)]),
        "consts": con,
        "sel": sel,
        "idb": np.eye(P).astype(np.dtype("bfloat16")),
    }
    nc = bacc.Bacc("TRN2", target_bir_lowering=False, num_devices=1)
    args = {}
    for name, a in arrays.items():
        arrays[name] = a = np.ascontiguousarray(a)
        args[name] = nc.dram_tensor(name, a.shape, mybir.dt.from_np(a.dtype), kind="ExternalInput").ap()
    out = nc.dram_tensor("out", (B * L, D), F32, kind="ExternalOutput").ap()
    decoder_layer(nc, out=out, **args)
    got = run_bass_kernel_spmd(nc, [arrays], core_ids=[0])
    return got.results[0]["out"].reshape(B, L, D)
```

```python
from contextlib import ExitStack

import concourse.bass as bass
from concourse import mybir

ALU = mybir.AluOpType
ACT = mybir.ActivationFunctionType
F32 = mybir.dt.float32
BF16 = mybir.dt.bfloat16
U32 = mybir.dt.uint32
F32R = mybir.dt.float32r
AX = mybir.AxisListType

P = 128
D = 128
B, L = 16, 64
TILES = B * L // P
CHUNKS = TILES // 2
J, HD = 16, 8
QUAD = 4
GROUPS = 8
PAIRS = GROUPS // 2
S = 64
NB = 4
NF = 32
TOP = 4
EXPERTS, HIDDEN = 8, 256
EPS = 1e-5
SCALE = float(HD) ** -0.5
HIGH = 0xFFFFF000

W_K, W_V, W_O2, W_Q, W_O, W_GATE = 0, 128, 256, 384, 512, 640
R_BQKV, R_BO, R_EBIAS, R_LEN = 0, 384, 512, 520
C_ID = 0
C_ODD = 128
C_POW = C_ODD + 2
C_FWD = C_POW + 2
C_INV = C_FWD + D
C_REL = C_INV + 3 * NB * L
C_HEAD = C_REL + 8
C_IOTA = C_HEAD + J
C_LEN = C_IOTA + 8


SLOTS = {
    "cdft": (7.36, 11.02, 19.21, 22.15),
    "cproj": (10.93, 19.62, 19.76, 28.54),
    "st1": (-2.86, 5.79, 14.36, 21.8),
    "nm1": (0.66, 6.88, 15.87, 23.14),
    "xt": (1.79, 8.04, 16.95, 24.45),
    "qkv": (2.52, 8.96, 17.9, 25.12),
    "ft": (2.82, 9.91, 18.67, 26.21),
    "fv": (3.49, 10.36, 19.06, 26.54),
    "score": (6.08, 12.16, 21.11, 28.43),
    "exp": (6.8, 13.25, 23.07, 29.92),
    "flip": (8.28, 14.93, 25.34, 30.94),
    "vtr": (12.46, 19.52, 27.68, 35.9),
    "pv": (17.82, 22.22, 29.91, 37.43),
    "vt2": (18.81, 22.68, 31.45, 38.93),
    "wo": (19.74, 24.09, 32.52, 39.56),
    "st2": (20.09, 24.32, 36.07, 40.45),
    "nm2": (21.2, 25, 36.44, 43.31),
    "dft": (22.26, 26.25, 37.27, 44.39),
    "qp": (22.43, 26.77, 37.91, 44.78),
    "corr": (23.46, 28.08, 39.54, 45.88),
    "g": (25.95, 30.17, 41.8, 48.67),
    "ov": (26.79, 30.91, 43.32, 49.82),
    "y2": (27.28, 32.12, 44.4, 50.52),
    "st3": (28.98, 33.65, 45.19, 50.86),
    "nm3": (29.8, 34.36, 45.37, 53.19),
    "xt3": (30.92, 36.35, 47.52, 54.75),
    "gate": (31.42, 37.17, 47.81, 55.24),
    "wt": (32.76, 38.36, 50.02, 57.56),
    "wb": (33.11, 38.87, 50.85, 62.05),
}
PARTS = {"qkv": 2, "ft": 2, "fv": 2, "score": QUAD, "exp": QUAD, "flip": QUAD, "vtr": 2, "wb": EXPERTS // 2, "wsplit": EXPERTS // 2}
PART_STEP = {"qkv": 0.98, "ft": 0.9, "score": 1.11, "vtr": 0.88, "exp": 0.99, "flip": 0.99, "wb": 0.91, "fv": 1.26, "wsplit": 0.05}
UNIT = {"up": 0.71, "sq": 1.79, "down": 3.07}
UNIT_START = (33.1, 42.71, 51.17, 71.52)
UNIT_STEP = (0.91, 0.61, 0.64, 0.1)
CHUNK_END = {"acc": 3.93, "fin": 8.36}
WSPLIT = 17.11


def steps():
    found = [(WSPLIT + PART_STEP["wsplit"] * part, "wsplit", 0, part) for part in range(PARTS["wsplit"])]
    for name, slots in SLOTS.items():
        for a in range(CHUNKS):
            for part in range(PARTS.get(name, 1)):
                found.append((slots[a] + PART_STEP.get(name, 1) * part, name, a, part))
    for a in range(CHUNKS):
        for e in range(EXPERTS):
            for name, slot in UNIT.items():
                found.append((UNIT_START[a] + UNIT_STEP[a] * e + slot, name, EXPERTS * a + e, 0))
        for name, slot in CHUNK_END.items():
            found.append((UNIT_START[a] + UNIT_STEP[a] * (EXPERTS - 1) + slot, name, a, 0))
    found.sort(key=lambda x: round(x[0], 4))
    return [x[1:] for x in found]


STEPS = steps()


RING = 7
TURN = ("xt", "cdft", "cproj", "vtr", "vt2", "dft", "g", "ov", "xt3", "gate", "wt", "wb")
WORK = ("qkv", "pv", "wo", "qp", "corr", "y2", "fin")


def numbered(names):
    return {step: n for n, step in enumerate(x for x in STEPS if x[0] in names)}


def decoder_layer(nc, x, ctxt, w_qkv, w_mid, w_up, w_down, rows, consts, sel, idb, out):
    with ExitStack() as ctx:
        def sb(name, shape, dt=F32):
            return ctx.enter_context(nc.sbuf_tensor(name, shape, dt))

        def sem(name):
            return ctx.enter_context(nc.semaphore(name))

        x_sb = sb("x_sb", [P, TILES, D])
        c_sb = sb("c_sb", [P, TILES, D])
        x12 = sb("x12", [P, TILES, D])
        xn = sb("xn", [P, TILES, D])
        stat = sb("stat", [P, 3 * CHUNKS, 2, 6])
        mv = sb("mv", [P, 3 * CHUNKS, 2, 2])
        rstd = sb("rstd", [P, 3 * CHUNKS, 2])
        xt = sb("xt", [P, 2, 2 * P])
        wqkv_sb = sb("wqkv_sb", [P, 3 * D])
        wmid_sb = sb("wmid_sb", [P, W_GATE + EXPERTS])
        wup_sb = sb("wup_sb", [P, EXPERTS, HIDDEN])
        whi = sb("whi", [P, EXPERTS, HIDDEN], F32R)
        wlo = sb("wlo", [P, EXPERTS, HIDDEN], F32R)
        wdn_sb = sb("wdn_sb", [P, EXPERTS, 2, D])
        row_sb = sb("row_sb", [P, R_LEN])
        con = sb("con", [P, C_LEN])
        identb = sb("identb", [P, P], BF16)
        selb = sb("selb", [3 * EXPERTS, EXPERTS, P], BF16)
        nat = sb("nat", [P, 2, 3, J, 32])
        vrow = sb("vrow", [P, 2, D])
        feat = sb("feat", [P, 3, 2, 2, GROUPS, S])
        negm = sb("negm", [P, CHUNKS, QUAD, GROUPS])
        praw = sb("praw", [P, QUAD, GROUPS * S])
        prob = sb("prob", [P, 2, QUAD, PAIRS, P])
        vkey = sb("vkey", [P, 2, 2, PAIRS, P])
        onat = sb("onat", [P, J, 32])
        rden = sb("rden", [P, J, 2])
        vals = sb("vals", [P, 2, 2, D])
        valsT = sb("valsT", [P, 2, 2 * P])
        cx = sb("cx", [P, 2, 4 * P])
        kv = sb("kv", [P, CHUNKS, 4 * P])
        qf = sb("qf", [P, 2, 2 * P])
        prod = sb("prod", [P, 2, 4, D])
        topv = sb("topv", [P, CHUNKS, NB, 8])
        topi = sb("topi", [P, CHUNKS, NB, 8], U32)
        topr = sb("topr", [P, CHUNKS, NB, 8], U32)
        dif = sb("dif", [P, CHUNKS, NB, TOP])
        ex = sb("ex", [P, CHUNKS, NB, TOP])
        exs = sb("exs", [P, CHUNKS, NB])
        exr = sb("exr", [P, CHUNKS, NB])
        wgt = sb("wgt", [P, CHUNKS, NB, TOP])
        hit = sb("hit", [P, NB, 8, TOP])
        w8 = sb("w8", [P, CHUNKS, NB, 8])
        mix = sb("mix", [P, 2, NB, J, 8])
        mixT = sb("mixT", [P, NB, D])
        ovT = sb("ovT", [P, 2, NB, HD, J // 2])
        xn3T = sb("xn3T", [P, 2, 2 * P])
        xtop = sb("xtop", [P, 2, 2 * P], U32)
        xhi = sb("xhi", [P, 2, 2 * P], F32R)
        xlo = sb("xlo", [P, 2, 2 * P], F32R)
        eg = sb("eg", [P, CHUNKS, 2, EXPERTS])
        eg1 = sb("eg1", [P, CHUNKS, 2, EXPERTS])
        gate = sb("gate", [P, CHUNKS, 2, EXPERTS])
        biased = sb("biased", [P, CHUNKS, 2, EXPERTS])
        bestv = sb("bestv", [P, CHUNKS, 2, 8])
        besti = sb("besti", [P, CHUNKS, 2, 8], U32)
        pick = sb("pick", [P, CHUNKS, 2, EXPERTS, 2])
        picked = sb("picked", [P, CHUNKS, 2, EXPERTS])
        wtok = sb("wtok", [P, CHUNKS, 2, EXPERTS])
        rest = sb("rest", [P, CHUNKS, 2, 2, EXPERTS])
        wparts = sb("wparts", [P, CHUNKS, 2, 3 * EXPERTS], BF16)
        wT = sb("wT", [3 * EXPERTS, 2, 2 * P], BF16)
        wb_sb = sb("wb_sb", [P, 2, EXPERTS, 2 * P])
        wtop = wb_sb[:, 1].bitcast(U32)
        rel = sb("rel", [P, 2, 4 * P])
        hid = sb("hid", [P, 3, 4 * P])
        accT = sb("accT", [P, 2 * P])
        fin = x_sb

        ps = ctx.enter_context(nc.psum_tensor("ps", [P, 8, 512], F32))
        acc_ps = ps[:, RING, :]
        turn_at, work_at, ring_at = numbered(TURN), numbered(WORK), numbered(TURN + WORK + ("score", "flip", "up"))

        def psum(name, a, part=0):
            return ps[:, ring_at[(name, a, part)] % RING, :]

        ld_x0, ld_x = sem("ld_x0"), sem("ld_x")
        ld_c = sem("ld_c")
        ld_id, ld_con, ld_wqkv, ld_mid, ld_up, ld_dn, ld_row, ld_sel = (
            sem(n) for n in ("ld_id", "ld_con", "ld_wqkv", "ld_mid", "ld_up", "ld_dn", "ld_row", "ld_sel"))
        zeroed = sem("zeroed")
        xb_ready = sem("xb_ready")
        stats_ready = sem("stats_ready")
        agg = sem("agg")
        veps_ready = sem("veps_ready")
        rstd_ready = sem("rstd_ready")
        norm_ready = sem("norm_ready")
        turn_full = sem("turn_full")
        turn_free = sem("turn_free")
        work_full = sem("work_full")
        work_free = sem("work_free")
        score_full = sem("score_full")
        score_free = sem("score_free")
        max_ready = sem("max_ready")
        exp_ready = sem("exp_ready")
        flip_full = sem("flip_full")
        flip_free = sem("flip_free")
        vnat_ready = sem("vnat_ready")
        nat_ready = sem("nat_ready")
        qkt_ready = sem("qkt_ready")
        vt_ready = sem("vt_ready")
        rden_ready = sem("rden_ready")
        vals_ready = sem("vals_ready")
        prod_ready = sem("prod_ready")
        prodc_ready = sem("prodc_ready")
        top_val = sem("top_val")
        dif_ready = sem("dif_ready")
        ex_ready = sem("ex_ready")
        tk = sem("tk")
        w8_ready = sem("w8_ready")
        mix_ready = sem("mix_ready")
        best_ready = sem("best_ready")
        split_ready = sem("split_ready")
        z_full = sem("z_full")
        z_free = sem("z_free")
        hid_ready = sem("hid_ready")
        down_done = sem("down_done")
        acct_ready = sem("acct_ready")
        wtop_ready, whi_ready, wlo_ready = sem("wtop_ready"), sem("whi_ready"), sem("wlo_ready")
        xtop_ready, xhi_ready, xlo_ready = sem("xtop_ready"), sem("xhi_ready"), sem("xlo_ready")
        stored = sem("stored")

        ident = con[:, C_ID:C_ID + P]
        block = ctx.enter_context(nc.Block())

        @block.sync
        def _(sp):
            xv = x.rearrange("(t p) d -> p t d", p=P)
            ov = out.rearrange("(t p) d -> p t d", p=P)
            cv = ctxt.rearrange("(t p) d -> p t d", p=P)
            sp.dma_start(x_sb[:, 0:2, :], xv[:, 0:2, :]).then_inc(ld_x0, 16)
            sp.dma_start(wqkv_sb[:], w_qkv).then_inc(ld_wqkv, 16)
            sp.dma_start(c_sb[:], cv).then_inc(ld_c, 16)
            sp.dma_start(x_sb[:, 2:TILES, :], xv[:, 2:TILES, :]).then_inc(ld_x, 16)
            sp.dma_start(wup_sb[:].rearrange("p e h -> p (e h)"), w_up).then_inc(ld_up, 16)
            sp.dma_start(wdn_sb[:].rearrange("p e c n -> p (e c n)"), w_down).then_inc(ld_dn, 16)
            sp.dma_start(selb[:].rearrange("k e p -> k (e p)"), sel).then_inc(ld_sel, 16)
            sp.dma_start(identb[:], idb).then_inc(ld_sel, 16)
            for name, a, part in STEPS:
                if name == "fin":
                    sp.wait_ge(work_free, work_at[("fin", a, 0)] + 1)
                    sp.dma_start(ov[:, 2 * a:2 * a + 2, :], fin[:, 2 * a:2 * a + 2, :]).then_inc(stored, 16)
            sp.wait_ge(stored, 16 * CHUNKS)

        @block.gpsimd
        def _(pool):
            nc.gpsimd.memset(nat[:], 0.0).then_inc(zeroed, 1)
            pool.wait_ge(zeroed, 1)
            pool.wait_ge(ld_id, 16)
            parity = con[:, C_ODD:C_ODD + 2].unsqueeze(1)
            for t in range(2):
                nc.gpsimd.tensor_copy(nat[:, t, 2, :, 2 * HD:2 * HD + 2], parity.broadcast_to([P, J, 2])).then_inc(zeroed, 1)

            def rsqrt(n):
                pool.wait_ge(stats_ready, 2 * (n + 1))
                if n == 0:
                    pool.wait_ge(ld_id, 16)
                nc.gpsimd.tensor_scalar(rstd[:, n, :], mv[:, n, :, 1], EPS, None, ALU.add).then_inc(veps_ready, 1)
                pool.wait_ge(veps_ready, n + 1)
                nc.gpsimd.tensor_tensor(rstd[:, n, :], rstd[:, n, :], con[:, C_POW:C_POW + 2], ALU.pow).then_inc(rstd_ready, 1)

            norms = 0
            for name, a, part in STEPS:
                if name in ("st1", "st2", "st3"):
                    rsqrt(norms)
                    norms += 1
                if name == "score" and a == 0 and part == 0:
                    pool.wait_ge(ld_row, 16)
                    pool.wait_ge(ld_x, 16)
                    nc.gpsimd.tensor_tensor(x12[:], x_sb[:], row_sb[:, R_BO:R_BO + D].unsqueeze(1).broadcast_to([P, TILES, D]),
                                            ALU.add).then_inc(xb_ready, 1)
                if name == "qkv":
                    t = part
                    pool.wait_ge(work_free, work_at[("qkv", a, t)] + 1)
                    if a:
                        pool.wait_ge(vt_ready, 2 * (a - 1) + t + 1)
                    nc.gpsimd.tensor_tensor(
                        nat[:, t, 2, :, 0:2 * HD].rearrange("p j (g d) -> p j g d", d=HD),
                        vrow[:, t].rearrange("p (j d) -> p j d", d=HD).unsqueeze(2).broadcast_to([P, J, 2, HD]),
                        parity.unsqueeze(3).broadcast_to([P, J, 2, HD]), ALU.mult).then_inc(vnat_ready, 1)
                if name == "wsplit":
                    two = slice(2 * part, 2 * part + 2)
                    pool.wait_ge(wtop_ready, part + 1)
                    nc.gpsimd.tensor_tensor(wlo[:, two], wup_sb[:, two], wtop[:, two].bitcast(F32), ALU.subtract).then_inc(wlo_ready, 1)
                if name == "xt3":
                    pool.wait_ge(xtop_ready, a + 1)
                    if a >= 2:
                        pool.wait_ge(z_full, EXPERTS * (a - 1))
                    nc.gpsimd.tensor_copy(xhi[:, a % 2, :], xtop[:, a % 2, :].bitcast(F32)).then_inc(xhi_ready, 1)
                    nc.gpsimd.tensor_tensor(xlo[:, a % 2, :], xn3T[:, a % 2, :], xtop[:, a % 2, :].bitcast(F32),
                                            ALU.subtract).then_inc(xlo_ready, 1)
                if name == "corr":
                    pool.wait_ge(w8_ready, a + 1)
                    if a >= 2:
                        pool.wait_ge(turn_full, turn_at[("g", a - 2, 0)] + 1)
                    for b in range(NB):
                        nc.gpsimd.tensor_tensor(
                            mix[:, a % 2, b], w8[:, a, b, :].unsqueeze(1).broadcast_to([P, J, 8]),
                            con[:, C_HEAD:C_HEAD + J].unsqueeze(2).broadcast_to([P, J, 8]), ALU.mult).then_inc(mix_ready, 1)

        @block.scalar
        def _(act):
            act.dma_start(con[:, 0:C_FWD], consts[:, 0:C_FWD]).then_inc(ld_id, 16)
            act.dma_start(row_sb[:], rows.partition_broadcast(P)).then_inc(ld_row, 16)
            act.dma_start(con[:, C_FWD:C_LEN], consts[:, C_FWD:C_LEN]).then_inc(ld_con, 16)
            act.dma_start(wmid_sb[:], w_mid).then_inc(ld_mid, 16)

            def turn(step, dst, src):
                act.wait_ge(turn_full, turn_at[step] + 1)
                nc.scalar.copy(dst, src).then_inc(turn_free, 1)

            for step in STEPS:
                name, a, part = step
                turn_ps = psum(*step) if name in TURN else None
                if name == "xt":
                    if a >= 2:
                        act.wait_ge(work_full, work_at[("qkv", a - 2, 1)] + 1)
                    turn(step, xt[:, a % 2, :], turn_ps[:, 0:2 * P])
                if name == "cdft":
                    if a >= 2:
                        act.wait_ge(turn_full, turn_at[("cproj", a - 2, 0)] + 1)
                    turn(step, cx[:, a % 2, :], turn_ps)
                if name == "cproj":
                    turn(step, kv[:, a, :], turn_ps)
                if name == "vtr":
                    if a >= 2:
                        act.wait_ge(work_full, work_at[("pv", a - 2, 0)] + 1)
                    turn(step, vkey[:, a % 2, part], turn_ps.rearrange("p (i n) -> p i n", n=P))
                if name == "exp":
                    act.wait_ge(score_free, QUAD * a + part + 1)
                    nc.scalar.activation(praw[:, part], praw[:, part], ACT.Exp, scale=SCALE).then_inc(exp_ready, 1)
                if name == "flip":
                    act.wait_ge(flip_full, QUAD * a + part + 1)
                    if a >= 2:
                        act.wait_ge(work_full, work_at[("pv", a - 2, 0)] + 1)
                    nc.scalar.copy(prob[:, a % 2, part], psum(*step).rearrange("p (i n) -> p i n", n=P)).then_inc(flip_free, 1)
                if name == "vt2":
                    if a >= 2:
                        act.wait_ge(work_full, work_at[("wo", a - 2, 0)] + 1)
                    act.wait_ge(turn_full, turn_at[step] + 1)
                    for t in range(2):
                        for g in range(2):
                            last = nc.scalar.copy(
                                valsT[:, a % 2, P * t:P * (t + 1)].rearrange("p (c g r) -> p c g r", g=2, r=4)[:, :, g],
                                turn_ps[:, P * g:P * (g + 1)].rearrange("p (q t c) -> p t q c", q=QUAD, t=2)[:, t].rearrange(
                                    "p q (i r) -> p q i r", r=4))
                    last.then_inc(turn_free, 1)
                if name == "dft":
                    if a >= 2:
                        act.wait_ge(work_full, work_at[("qp", a - 2, 0)] + 1)
                    turn(step, qf[:, a % 2, :], turn_ps[:, 0:2 * P])
                if name == "corr":
                    act.wait_ge(dif_ready, a + 1)
                    nc.scalar.activation(ex[:, a], dif[:, a], ACT.Exp).then_inc(ex_ready, 1)
                if name == "g":
                    if a >= 1:
                        act.wait_ge(turn_full, turn_at[("ov", a - 1, 0)] + 1)
                    turn(step, mixT[:], turn_ps.rearrange("p (b n) -> p b n", n=D))
                if name == "ov":
                    if a >= 2:
                        act.wait_ge(work_full, work_at[("y2", a - 2, 0)] + 1)
                    turn(step, ovT[:, a % 2].rearrange("p b d h -> p b h d"),
                         turn_ps[:, 0:NB * L].rearrange("p (b h d) -> p b h d", b=NB, d=HD))
                if name == "xt3":
                    if a >= 2:
                        act.wait_ge(turn_full, turn_at[("gate", a - 2, 0)] + 1)
                        act.wait_ge(xlo_ready, a - 1)
                    turn(step, xn3T[:, a % 2, :], turn_ps[:, 0:2 * P])
                if name == "gate":
                    act.wait_ge(turn_full, turn_at[step] + 1)
                    nc.scalar.activation(eg[:, a].rearrange("p t e -> p (t e)"), turn_ps[:, 0:2 * EXPERTS], ACT.Exp,
                                         scale=-1.0).then_inc(turn_free, 1)
                if name == "wt":
                    if a >= 2:
                        act.wait_ge(turn_full, turn_at[("wb", a - 2, EXPERTS // 2 - 1)] + 1)
                    turn(step, wT[:, a % 2, :], turn_ps.bitcast(BF16)[0:3 * EXPERTS, 0:2 * P])
                if name == "wsplit":
                    two = slice(2 * part, 2 * part + 2)
                    act.wait_ge(wtop_ready, part + 1)
                    nc.scalar.copy(whi[:, two], wtop[:, two].bitcast(F32)).then_inc(whi_ready, 1)
                if name == "wb":
                    if a == 1:
                        act.wait_ge(whi_ready, EXPERTS // 2)
                        act.wait_ge(wlo_ready, EXPERTS // 2)
                    if a >= 2:
                        act.wait_ge(z_free, EXPERTS * (a - 2) + 2 * part + 2)
                    turn(step, wb_sb[:, a % 2, 2 * part:2 * part + 2, :], turn_ps.rearrange("p (e t) -> p e t", e=2))
                if name == "sq":
                    act.wait_ge(z_free, a + 1)
                    if a >= 3:
                        act.wait_ge(down_done, a - 2)
                    nc.scalar.activation(hid[:, a % 3, :], rel[:, a % 2, :], ACT.Square).then_inc(hid_ready, 1)
                if name == "acc":
                    act.wait_ge(down_done, EXPERTS * (a + 1))
                    if a:
                        act.wait_ge(work_full, work_at[("fin", a - 1, 0)] + 1)
                    nc.scalar.copy(accT[:], acc_ps[:, 0:2 * P]).then_inc(acct_ready, 1)

        @block.vector
        def _(dve):
            chain = [0]

            def link(ins):
                chain[0] += 1
                ins.then_inc(tk, 1)
                dve.wait_ge(tk, chain[0])

            def stats(n, src, a):
                for t in range(2):
                    nc.vector.bn_stats(stat[:, n, t, :], src[:, 2 * a + t, :]).then_inc(agg, 1)
                for t in range(2):
                    dve.wait_ge(agg, 2 * n + t + 1)
                    nc.vector.bn_aggr(mv[:, n, t, :], stat[:, n, t, :]).then_inc(stats_ready, 1)

            def normalise(n, dst, src, a):
                dve.wait_ge(rstd_ready, n + 1)
                dve.wait_ge(stats_ready, 2 * (n + 1))
                for t in range(2):
                    nc.vector.tensor_scalar(dst[:, 2 * a + t, :], src[:, 2 * a + t, :], mv[:, n, t, 0:1], rstd[:, n, t:t + 1],
                                            ALU.subtract, ALU.mult).then_inc(norm_ready, 1)

            def work(name, a, part=0):
                use = work_at[(name, a, part)]
                dve.wait_ge(work_full, use + 1)
                return psum(name, a, part)

            norm_no = {}
            for name, a, part in STEPS:
                if name in ("st1", "st2", "st3"):
                    if name == "st1":
                        dve.wait_ge(ld_x if a else ld_x0, 16)
                    norm_no[(name[2], a)] = len(norm_no)
                    stats(norm_no[(name[2], a)], {"1": x_sb, "2": x12, "3": x12}[name[2]], a)
                if name == "nm1":
                    normalise(norm_no[("1", a)], xn, x_sb, a)
                if name == "qkv":
                    t = part
                    if a == 0:
                        dve.wait_ge(zeroed, 3)
                        dve.wait_ge(ld_row, 16)
                    if a > 0:
                        dve.wait_ge(qkt_ready, 4 * (a - 1) + 2 * (t + 1))
                    bias = row_sb[:, R_BQKV:R_BQKV + 3 * D].rearrange("p (c d) -> p c d", d=HD)
                    proj = work(name, a, t)[:, 0:3 * D].rearrange("p (c d) -> p c d", d=HD)
                    nc.vector.tensor_tensor(nat[:, t, 0:2, :, 0:HD].rearrange("p c j d -> p (c j) d"),
                                            proj[:, 0:2 * J], bias[:, 0:2 * J], ALU.add).then_inc(nat_ready, 1)
                    if a > 0:
                        dve.wait_ge(vnat_ready, 2 * (a - 1) + t + 1)
                    nc.vector.tensor_tensor(vrow[:, t].rearrange("p (j d) -> p j d", d=HD), proj[:, 2 * J:3 * J],
                                            bias[:, 2 * J:3 * J], ALU.add).then_inc(work_free, 1)
                if name == "ft":
                    t = part
                    dve.wait_ge(nat_ready, 2 * a + t + 1)
                    if a >= 2:
                        dve.wait_ge(score_full, QUAD * (a - 1))
                    for c in range(2):
                        nc.vector.transpose(feat[:, c, a % 2, t].rearrange("p h (j r) -> p j h r", j=J),
                                            nat[:, t, c, :, :]).then_inc(qkt_ready, 1)
                if name == "fv":
                    t = part
                    dve.wait_ge(vnat_ready, 2 * a + t + 1)
                    if a >= 2:
                        dve.wait_ge(turn_full, turn_at[("vtr", a - 2, 1)] + 1)
                    nc.vector.transpose(feat[:, 2, a % 2, t].rearrange("p h (j r) -> p j h r", j=J),
                                        nat[:, t, 2, :, :]).then_inc(vt_ready, 1)
                if name == "score":
                    dve.wait_ge(score_full, QUAD * a + part + 1)
                    if a:
                        dve.wait_ge(flip_full, QUAD * (a - 1) + part + 1)
                    s_ps = psum(name, a, part).rearrange("p (h s) -> p h s", s=S)
                    nc.vector.tensor_reduce(negm[:, a, part, :], s_ps, AX.X, ALU.max, negate=True).then_inc(max_ready, 1)
                    dve.wait_ge(max_ready, QUAD * a + part + 1)
                    nc.vector.tensor_tensor(praw[:, part].rearrange("p (h s) -> p h s", s=S), s_ps,
                                            negm[:, a, part, :].unsqueeze(2).broadcast_to([P, GROUPS, S]),
                                            ALU.add).then_inc(score_free, 1)
                if name == "pv":
                    if a:
                        dve.wait_ge(vals_ready, 2 * a)
                    nc.vector.transpose(onat[:], work(name, a).rearrange("p (h j r) -> p j h r", h=GROUPS, j=J)).then_inc(work_free, 1)
                    dve.wait_ge(work_free, work_at[(name, a, 0)] + 1)
                    nc.vector.reciprocal(rden[:], onat[:, :, 2 * HD:2 * HD + 2]).then_inc(rden_ready, 1)
                    dve.wait_ge(rden_ready, a + 1)
                    if a >= 2:
                        dve.wait_ge(turn_full, turn_at[("vt2", a - 2, 0)] + 1)
                    for g in range(2):
                        nc.vector.tensor_tensor(
                            vals[:, a % 2, g].rearrange("p (j d) -> p j d", d=HD), onat[:, :, HD * g:HD * (g + 1)],
                            rden[:, :, g:g + 1].broadcast_to([P, J, HD]), ALU.mult).then_inc(vals_ready, 1)
                if name == "wo":
                    if a == 0:
                        dve.wait_ge(xb_ready, 1)
                    both = x12[:, 2 * a:2 * a + 2, :]
                    nc.vector.tensor_tensor(both, work(name, a)[:, 0:2 * D].rearrange("p (t n) -> p t n", n=D), both,
                                            ALU.add).then_inc(work_free, 1)
                    dve.wait_ge(work_free, work_at[(name, a, 0)] + 1)
                if name == "nm2":
                    dve.wait_ge(turn_full, turn_at[("xt", a, 0)] + 1)
                    normalise(norm_no[("2", a)], xn, x12, a)
                if name == "qp":
                    if a >= 2:
                        dve.wait_ge(work_full, work_at[("corr", a - 2, 0)] + 1)
                    dve.wait_ge(turn_free, turn_at[("cproj", a, 0)] + 1)
                    spec = work(name, a)
                    nc.vector.tensor_tensor(prod[:, a % 2, 0:2, :], spec[:, 0:2 * D].rearrange("p (i c) -> p i c", c=D),
                                            kv[:, a, 0:2 * D].rearrange("p (i c) -> p i c", c=D), ALU.mult).then_inc(prod_ready, 1)
                    nc.vector.tensor_tensor(prod[:, a % 2, 3, :], spec[:, 0:D], kv[:, a, D:2 * D], ALU.mult).then_inc(prodc_ready, 1)
                    nc.vector.tensor_tensor(prod[:, a % 2, 2, :], spec[:, D:2 * D], kv[:, a, 0:D], ALU.mult).then_inc(work_free, 1)
                    dve.wait_ge(prodc_ready, 2 * a + 1)
                    dve.wait_ge(work_free, work_at[(name, a, 0)] + 1)
                    nc.vector.tensor_tensor(prod[:, a % 2, 2, :], prod[:, a % 2, 2, :], prod[:, a % 2, 3, :],
                                            ALU.subtract).then_inc(prodc_ready, 1)
                if name == "corr":
                    corr = work(name, a)[:, 0:NB * L].rearrange("p (b s) -> p b s", s=L)
                    for b in range(NB):
                        nc.vector.max(topv[:, a, b, :], corr[:, b, :]).then_inc(top_val, 1)
                    for b in range(NB):
                        dve.wait_ge(top_val, NB * a + b + 1)
                        last = nc.vector.max_index(topi[:, a, b, :], topv[:, a, b, :], corr[:, b, :])
                    last.then_inc(work_free, 1)
                    dve.wait_ge(work_free, work_at[(name, a, 0)] + 1)
                    nc.vector.tensor_tensor(dif[:, a], topv[:, a, :, 0:TOP], topv[:, a, :, 0:1].broadcast_to([P, NB, TOP]),
                                            ALU.subtract).then_inc(dif_ready, 1)
                    if a:
                        dve.wait_ge(w8_ready, a)
                    link(nc.vector.tensor_single_scalar(topr[:, a], topi[:, a], HD - 1, ALU.bitwise_and))
                    if a == 0:
                        dve.wait_ge(ld_con, 16)
                    link(nc.vector.tensor_tensor(
                        hit[:], topr[:, a, :, 0:TOP].unsqueeze(2).broadcast_to([P, NB, 8, TOP]),
                        con[:, C_REL:C_REL + 8].unsqueeze(1).unsqueeze(3).broadcast_to([P, NB, 8, TOP]), ALU.is_equal))
                    dve.wait_ge(ex_ready, a + 1)
                    link(nc.vector.tensor_reduce(exs[:, a], ex[:, a], AX.X, ALU.add))
                    link(nc.vector.reciprocal(exr[:, a], exs[:, a]))
                    link(nc.vector.tensor_tensor(wgt[:, a], ex[:, a], exr[:, a].unsqueeze(2).broadcast_to([P, NB, TOP]), ALU.mult))
                    link(nc.vector.tensor_tensor(hit[:], hit[:], wgt[:, a].unsqueeze(2).broadcast_to([P, NB, 8, TOP]), ALU.mult))
                    nc.vector.tensor_reduce(w8[:, a], hit[:], AX.X, ALU.add).then_inc(w8_ready, 1)
                if name == "y2":
                    dve.wait_ge(work_free, work_at[("wo", a, 0)] + 1)
                    nc.vector.tensor_tensor(x12[:, 2 * a:2 * a + 2, :], work(name, a)[:, 0:2 * D].rearrange("p (t n) -> p t n", n=D),
                                            x12[:, 2 * a:2 * a + 2, :], ALU.add).then_inc(work_free, 1)
                    dve.wait_ge(work_free, work_at[(name, a, 0)] + 1)
                if name == "nm3":
                    dve.wait_ge(turn_full, turn_at[("dft", a, 0)] + 1)
                    normalise(norm_no[("3", a)], xn, x12, a)
                if name == "xt3":
                    dve.wait_ge(turn_free, turn_at[(name, a, 0)] + 1)
                    if a >= 2:
                        dve.wait_ge(xhi_ready, a - 1)
                        dve.wait_ge(xlo_ready, a - 1)
                    nc.vector.tensor_single_scalar(xtop[:, a % 2, :], xn3T[:, a % 2, :].bitcast(U32), HIGH,
                                                   ALU.bitwise_and).then_inc(xtop_ready, 1)
                if name == "wsplit":
                    two = slice(2 * part, 2 * part + 2)
                    dve.wait_ge(ld_up, 16)
                    nc.vector.tensor_single_scalar(wtop[:, two], wup_sb[:, two].bitcast(U32), HIGH, ALU.bitwise_and).then_inc(wtop_ready, 1)
                if name == "gate":
                    dve.wait_ge(turn_free, turn_at[(name, a, 0)] + 1)
                    link(nc.vector.tensor_scalar(eg1[:, a], eg[:, a], 1.0, None, ALU.add))
                    link(nc.vector.reciprocal(gate[:, a], eg1[:, a]))
                    link(nc.vector.tensor_tensor(biased[:, a], gate[:, a],
                                                 row_sb[:, R_EBIAS:R_EBIAS + EXPERTS].unsqueeze(1).broadcast_to([P, 2, EXPERTS]), ALU.add))
                    for t in range(2):
                        nc.vector.max(bestv[:, a, t], biased[:, a, t]).then_inc(best_ready, 1)
                    for t in range(2):
                        dve.wait_ge(best_ready, 2 * a + t + 1)
                        last = nc.vector.max_index(besti[:, a, t], bestv[:, a, t], biased[:, a, t])
                    link(last)
                    link(nc.vector.tensor_tensor(
                        pick[:, a], besti[:, a, :, 0:2].unsqueeze(2).broadcast_to([P, 2, EXPERTS, 2]),
                        con[:, C_IOTA:C_IOTA + 8].unsqueeze(1).unsqueeze(3).broadcast_to([P, 2, EXPERTS, 2]), ALU.is_equal))
                    link(nc.vector.tensor_reduce(picked[:, a], pick[:, a], AX.X, ALU.add))
                    link(nc.vector.tensor_tensor(wtok[:, a], picked[:, a], gate[:, a], ALU.mult))
                    part = [wparts[:, a, :, EXPERTS * i:EXPERTS * (i + 1)] for i in range(3)]
                    link(nc.vector.tensor_copy(part[0], wtok[:, a]))
                    link(nc.vector.tensor_tensor(rest[:, a, 0], wtok[:, a], part[0], ALU.subtract))
                    link(nc.vector.tensor_copy(part[1], rest[:, a, 0]))
                    link(nc.vector.tensor_tensor(rest[:, a, 1], rest[:, a, 0], part[1], ALU.subtract))
                    nc.vector.tensor_copy(part[2], rest[:, a, 1]).then_inc(split_ready, 1)
                if name == "up":
                    c, e = divmod(a, EXPERTS)
                    dve.wait_ge(turn_free, turn_at[("wb", c, e // 2)] + 1)
                    dve.wait_ge(z_full, a + 1)
                    if a >= 2:
                        dve.wait_ge(hid_ready, a - 1)
                    w_bc = wb_sb[:, (a // EXPERTS) % 2, a % EXPERTS, :].unsqueeze(1).broadcast_to([P, 2, 2 * P])
                    nc.vector.scalar_tensor_tensor(rel[:, a % 2, :].rearrange("p (c t) -> p c t", c=2),
                                                   psum(name, a).rearrange("p (c t) -> p c t", c=2), 0.0, w_bc, ALU.max,
                                                   ALU.mult).then_inc(z_free, 1)
                if name == "fin":
                    nc.vector.tensor_tensor(fin[:, 2 * a:2 * a + 2, :], work(name, a)[:, 0:2 * P].rearrange("p (t n) -> p t n", n=D),
                                            x12[:, 2 * a:2 * a + 2, :], ALU.add).then_inc(work_free, 1)

        @block.tensor
        def _(pe):
            def bank(name, a, part=0):
                use = ring_at[(name, a, part)]
                if use >= RING:
                    last = ring_order[use - RING]
                    was, c, r = last
                    if was in TURN:
                        pe.wait_ge(turn_free, turn_at[last] + 1)
                    elif was in WORK:
                        pe.wait_ge(work_free, work_at[last] + 1)
                    elif was == "score":
                        pe.wait_ge(score_free, QUAD * c + r + 1)
                    elif was == "flip":
                        pe.wait_ge(flip_free, QUAD * c + r + 1)
                    else:
                        pe.wait_ge(z_free, c + 1)
                return psum(name, a, part)

            def turned(name, a):
                pe.wait_ge(turn_free, turn_at[(name, a, 0)] + 1)

            mm = nc.tensor.matmul
            ring_order = list(ring_at)
            norm_no = {}

            for name, a, part in STEPS:
                if name in ("nm1", "nm2", "nm3"):
                    norm_no[(name, a)] = len(norm_no) + 1
                if name in ("xt", "xt3"):
                    if name == "xt" and a == 0:
                        pe.wait_ge(ld_id, 16)
                    pe.wait_ge(norm_ready, 2 * norm_no[("nm1" if name == "xt" else "nm3", a)])
                    ps_t = bank(name, a)
                    for t in range(2):
                        last = nc.tensor.transpose(ps_t[:, P * t:P * (t + 1)], xn[:, 2 * a + t, :], ident)
                    last.then_inc(turn_full, 1)
                if name == "qkv":
                    if a == 0:
                        pe.wait_ge(ld_wqkv, 16)
                    turned("xt", a)
                    mm(bank(name, a, part)[:, 0:3 * D], xt[:, a % 2, P * part:P * (part + 1)], wqkv_sb[:], start=True,
                       stop=True).then_inc(work_full, 1)
                if name == "cdft":
                    if a == 0:
                        pe.wait_ge(ld_id, 16)
                        pe.wait_ge(ld_c, 16)
                        pe.wait_ge(ld_con, 16)
                    ps_t = bank(name, a)
                    spec = ps_t[:, 0:2 * P].rearrange("p (i t f) -> p i t f", i=2, t=2)
                    for t in range(2):
                        mm(spec[:, :, t, :], c_sb[:, 2 * a + t, :], con[:, C_FWD:C_FWD + 2 * 2 * NF].rearrange("p (i f) -> p i f", i=2),
                           start=True, stop=True)
                        last = nc.tensor.transpose(ps_t[:, 2 * P + P * t:2 * P + P * (t + 1)], c_sb[:, 2 * a + t, :], ident)
                    last.then_inc(turn_full, 1)
                if name == "cproj":
                    if a == 0:
                        pe.wait_ge(ld_mid, 16)
                    turned("cdft", a)
                    ps_s = bank(name, a)
                    for i in range(2):
                        mm(ps_s[:, D * i:D * (i + 1)], cx[:, a % 2, P * i:P * (i + 1)], wmid_sb[:, W_K:W_K + D], start=True, stop=True)
                    mm(ps_s[:, 2 * P:4 * P], wmid_sb[:, W_V:W_V + D], cx[:, a % 2, 2 * P:4 * P], start=True,
                       stop=True).then_inc(turn_full, 1)
                if name == "score":
                    if part == 0:
                        pe.wait_ge(qkt_ready, 4 * (a + 1))
                    s_ps, q = bank(name, a, part), 32 * part
                    for h in range(GROUPS):
                        for g in range(2):
                            cols = slice(S * g, S * (g + 1))
                            last = mm(s_ps[cols, S * h:S * (h + 1)], feat[q:q + HD, 0, a % 2, g, h, :],
                                      feat[q:q + HD, 1, a % 2, g, h, :], start=True, stop=True)
                    last.then_inc(score_full, 1)
                if name == "flip":
                    pe.wait_ge(exp_ready, QUAD * a + part + 1)
                    t_ps = bank(name, a, part)
                    for i in range(PAIRS):
                        last = nc.tensor.transpose(t_ps[:, P * i:P * (i + 1)], praw[:, part, P * i:P * (i + 1)], ident)
                    last.then_inc(flip_full, 1)
                if name == "vtr":
                    if part == 0:
                        pe.wait_ge(vt_ready, 2 * (a + 1))
                    ps_s = bank(name, a, part)
                    for i in range(PAIRS):
                        last = nc.tensor.transpose(ps_s[:, P * i:P * (i + 1)],
                                                   feat[:, 2, a % 2, part, 2 * i:2 * i + 2, :].rearrange("p h s -> p (h s)"), ident)
                    last.then_inc(turn_full, 1)
                if name == "pv":
                    pe.wait_ge(turn_free, turn_at[("vtr", a, 1)] + 1)
                    o_ps = bank(name, a)
                    for r in range(QUAD):
                        pe.wait_ge(flip_free, QUAD * a + r + 1)
                        for t in range(2):
                            for i in range(PAIRS):
                                last = mm(o_ps[32 * r:32 * r + 32, S * (PAIRS * t + i):S * (PAIRS * t + i + 1)],
                                          vkey[:, a % 2, t, i, 32 * r:32 * r + 32], prob[:, a % 2, r, i, S * t:S * (t + 1)],
                                          start=True, stop=True)
                    last.then_inc(work_full, 1)
                if name == "vt2":
                    pe.wait_ge(vals_ready, 2 * (a + 1))
                    ps_t = bank(name, a)
                    for t in range(2):
                        last = nc.tensor.transpose(ps_t[:, P * t:P * (t + 1)], vals[:, a % 2, t, :], ident)
                    last.then_inc(turn_full, 1)
                if name == "wo":
                    turned("vt2", a)
                    y_ps = bank(name, a)
                    for t in range(2):
                        last = mm(y_ps[:, D * t:D * (t + 1)], valsT[:, a % 2, P * t:P * (t + 1)], wmid_sb[:, W_O:W_O + D],
                                  start=True, stop=True)
                    last.then_inc(work_full, 1)
                if name == "dft":
                    pe.wait_ge(norm_ready, 2 * norm_no[("nm2", a)])
                    ps_t = bank(name, a)
                    spec = ps_t[:, 0:2 * P].rearrange("p (i t f) -> p i t f", i=2, t=2)
                    for t in range(2):
                        last = mm(spec[:, :, t, :], xn[:, 2 * a + t, :],
                                  con[:, C_FWD:C_FWD + 2 * 2 * NF].rearrange("p (i f) -> p i f", i=2), start=True, stop=True)
                    last.then_inc(turn_full, 1)
                if name == "qp":
                    turned("dft", a)
                    q_ps = bank(name, a)
                    for i in range(2):
                        last = mm(q_ps[:, D * i:D * (i + 1)], qf[:, a % 2, P * i:P * (i + 1)], wmid_sb[:, W_Q:W_Q + D],
                                  start=True, stop=True)
                    last.then_inc(work_full, 1)
                if name == "corr":
                    pe.wait_ge(prod_ready, a + 1)
                    pe.wait_ge(prodc_ready, 2 * (a + 1))
                    c_ps = bank(name, a)
                    for i in range(3):
                        last = mm(c_ps[:, 0:NB * L], prod[:, a % 2, i, :], con[:, C_INV + NB * L * i:C_INV + NB * L * (i + 1)],
                                  start=(i == 0), stop=(i == 2))
                    last.then_inc(work_full, 1)
                if name == "g":
                    ps_t = bank(name, a)
                    for b in range(NB):
                        pe.wait_ge(mix_ready, NB * a + b + 1)
                        last = nc.tensor.transpose(ps_t[:, D * b:D * (b + 1)], mix[:, a % 2, b].rearrange("p h e -> p (h e)"), ident)
                    last.then_inc(turn_full, 1)
                if name == "ov":
                    turned("g", a)
                    ps_t = bank(name, a)
                    for b in range(NB):
                        for odd in range(2):
                            last = mm(ps_t[L * odd:L * (odd + 1), L * b:L * (b + 1)], kv[:, a, 2 * P + L * b:2 * P + L * (b + 1)],
                                      mixT[:, b, :].rearrange("p (h o d) -> p o h d", o=2, d=HD)[:, odd], start=True, stop=True)
                    last.then_inc(turn_full, 1)
                if name == "y2":
                    turned("ov", a)
                    y_ps = bank(name, a)
                    for t in range(2):
                        last = mm(y_ps[:, D * t:D * (t + 1)], ovT[:, a % 2, 2 * t:2 * t + 2].rearrange("p b d h -> p (b d h)"),
                                  wmid_sb[:, W_O2:W_O2 + D], start=True, stop=True)
                    last.then_inc(work_full, 1)
                if name == "gate":
                    turned("xt3", a)
                    ps_t = bank(name, a)
                    for t in range(2):
                        last = mm(ps_t[:, EXPERTS * t:EXPERTS * (t + 1)], xn3T[:, a % 2, P * t:P * (t + 1)],
                                  wmid_sb[:, W_GATE:W_GATE + EXPERTS], start=True, stop=True)
                    last.then_inc(turn_full, 1)
                if name == "wt":
                    pe.wait_ge(split_ready, a + 1)
                    ps_t = bank(name, a).bitcast(BF16)
                    if a == 0:
                        pe.wait_ge(ld_sel, 32)
                    for t in range(2):
                        last = nc.tensor.transpose(ps_t[0:3 * EXPERTS, P * t:P * (t + 1)], wparts[:, a, t, :], identb[:])
                    last.then_inc(turn_full, 1)
                if name == "wb":
                    turned("wt", a)
                    ps_t = bank(name, a, part)
                    for i in range(2):
                        last = mm(ps_t[:, 2 * P * i:2 * P * (i + 1)], selb[:, 2 * part + i, :], wT[:, a % 2, :],
                                  start=True, stop=True)
                    last.then_inc(turn_full, 1)
                if name == "up":
                    c, e = divmod(a, EXPERTS)
                    if e == 0:
                        pe.wait_ge(xhi_ready, c + 1)
                        pe.wait_ge(xlo_ready, c + 1)
                    if c == 0:
                        pe.wait_ge(whi_ready, e // 2 + 1)
                        pe.wait_ge(wlo_ready, e // 2 + 1)
                    z_ps = bank(name, a)
                    for half in range(2):
                        for i, (w, r) in enumerate(((whi, xhi), (whi, xlo), (wlo, xhi))):
                            last = mm(z_ps[:, 2 * P * half:2 * P * (half + 1)], w[:, e, P * half:P * (half + 1)], r[:, c % 2, :],
                                      start=(i == 0), stop=(i == 2))
                    last.then_inc(z_full, 1)
                if name == "down":
                    c, e = divmod(a, EXPERTS)
                    if a == 0:
                        pe.wait_ge(ld_dn, 16)
                    if c and e == 0:
                        pe.wait_ge(acct_ready, c)
                    pe.wait_ge(hid_ready, a + 1)
                    for half in range(2):
                        last = mm(acc_ps[:, 0:2 * P], wdn_sb[:, e, half, :], hid[:, a % 3, 2 * P * half:2 * P * (half + 1)],
                                  start=(e == 0 and half == 0), stop=(e == EXPERTS - 1 and half == 1))
                    last.then_inc(down_done, 1)
                if name == "fin":
                    pe.wait_ge(acct_ready, a + 1)
                    f_ps = bank(name, a)
                    for t in range(2):
                        last = nc.tensor.transpose(f_ps[:, P * t:P * (t + 1)], accT[:, P * t:P * (t + 1)], ident)
                    last.then_inc(work_full, 1)


def constants():
    import numpy as np
    con = np.zeros((P, C_LEN), np.float64)
    con[:, C_ID:C_ID + P] = np.eye(P)
    con[:, C_ODD] = np.arange(P) // 4 % 2 == 0
    con[:, C_ODD + 1] = np.arange(P) // 4 % 2 == 1
    l, f = np.arange(L), np.arange(NF)
    ang = 2 * np.pi * np.outer(l, f) / L
    alt = np.where(l % 2 == 0, 1.0, -1.0)
    re, im = np.cos(ang), -np.sin(ang)
    im[:, 0] = alt
    for b in range(2):
        con[L * b:L * (b + 1), C_FWD + NF * b:C_FWD + NF * (b + 1)] = re
        con[L * b:L * (b + 1), C_FWD + 2 * NF + NF * b:C_FWD + 2 * NF + NF * (b + 1)] = im
    wre = 2 * np.cos(ang).T / L
    wre[0] = 1.0 / L
    wim = wre.copy()
    wim[0] = alt / L
    wx = -2 * np.sin(ang).T / L
    for b in range(NB):
        for i, w in enumerate((wre, wim, wx)):
            con[NF * b:NF * (b + 1), C_INV + NB * L * i + L * b:C_INV + NB * L * i + L * (b + 1)] = w
    c = np.arange(P)
    con[:, C_REL:C_REL + 8] = (c[:, None] - np.arange(8)) % 8
    con[:, C_HEAD:C_HEAD + J] = c[:, None] // HD == np.arange(J)
    con[:, C_IOTA:C_IOTA + 8] = np.arange(8)
    con[:, C_POW:C_POW + 2] = -0.5
    sel = np.zeros((3, EXPERTS, EXPERTS, P), np.float32)
    for e in range(EXPERTS):
        sel[:, e, e, :] = 1
    return con.astype(np.float32), sel.reshape(3 * EXPERTS, EXPERTS * P).astype(np.dtype("bfloat16"))


def kernel(x, ctx_1024, L0_attn_Wqkv, L0_attn_bqkv, L0_attn_Wo, L0_attn_bo, L0_xattn_wq, L0_xattn_wk, L0_xattn_wv,
           L0_xattn_wo, L0_ffn_gate_w, L0_ffn_w_up, L0_ffn_w_down, L0_ffn_expert_bias):
    import numpy as np
    import concourse.bacc as bacc
    from concourse.bass_utils import run_bass_kernel_spmd

    def regroup(w):
        return w.reshape(J, 3, HD, -1).transpose(1, 0, 2, 3).reshape(3 * D, -1)

    wq, wk, wv, wo = (np.asarray(w) for w in (L0_xattn_wq, L0_xattn_wk, L0_xattn_wv, L0_xattn_wo))
    con, sel = constants()
    arrays = {
        "x": np.asarray(x).reshape(B * L, D),
        "ctxt": np.asarray(ctx_1024).reshape(B * L, D),
        "w_qkv": regroup(np.asarray(L0_attn_Wqkv)).T,
        "w_mid": np.concatenate([wk, wv, wo, wq, np.asarray(L0_attn_Wo).T, np.asarray(L0_ffn_gate_w).T], axis=1),
        "w_up": np.asarray(L0_ffn_w_up).transpose(2, 0, 1).reshape(P, EXPERTS * HIDDEN),
        "w_down": np.asarray(L0_ffn_w_down).reshape(EXPERTS, D, 2, P).transpose(3, 0, 2, 1).reshape(P, EXPERTS * 2 * D),
        "rows": np.concatenate([regroup(np.asarray(L0_attn_bqkv)[:, None])[:, 0], np.asarray(L0_attn_bo),
                                np.asarray(L0_ffn_expert_bias)]),
        "consts": con,
        "sel": sel,
        "idb": np.eye(P).astype(np.dtype("bfloat16")),
    }
    nc = bacc.Bacc("TRN2", target_bir_lowering=False, num_devices=1)
    args = {}
    for name, a in arrays.items():
        arrays[name] = a = np.ascontiguousarray(a)
        args[name] = nc.dram_tensor(name, a.shape, mybir.dt.from_np(a.dtype), kind="ExternalInput").ap()
    out = nc.dram_tensor("out", (B * L, D), F32, kind="ExternalOutput").ap()
    decoder_layer(nc, out=out, **args)
    got = run_bass_kernel_spmd(nc, [arrays], core_ids=[0])
    return got.results[0]["out"].reshape(B, L, D)
```
